# Optimizing a Trainium2 kernel written in Bass

```python
import numpy as np
import jax
import jax.numpy as jnp

def _softmax(x, axis=-1):
    return jax.nn.softmax(x, axis=axis)

def _gelu(x):
    return jax.nn.gelu(x, approximate=True)

def _silu(x):
    return jax.nn.silu(x)

def _sigmoid(x):
    return jax.nn.sigmoid(x)

def _layernorm(x, axis=-1, eps=1e-05):
    m = jnp.mean(x, axis=axis, keepdims=True)
    v = jnp.var(x, axis=axis, keepdims=True)
    return (x - m) / jnp.sqrt(v + eps)

def _scatter_add(tgt, idx, src, axis=0):
    return tgt.at[idx].add(src)

def _segment_sum(src, seg, n):
    return jax.ops.segment_sum(src, seg, n)
kernel_name = 'mk_cond_seq_d1_seqx_r2_6d04ed'

def setup_inputs(seed: int=0):
    np.random.seed(seed)
    _w = jnp.asarray

    def _rec_inputs():
        import jax
        import jax.numpy as jnp
        _rk = jax.random.key(seed)
        x = -0.0002928 + 1 * jax.random.normal(jax.random.fold_in(_rk, 1), (16, 512, 512), jnp.float32)
        _lenS = 512 - jax.random.randint(jax.random.fold_in(_rk, 7), (16,), 0, max(1, 512 // 4) + 1, jnp.int32)
        _lenS2 = 512 - jax.random.randint(jax.random.fold_in(_rk, 8), (16,), 0, max(1, 512 // 4) + 1, jnp.int32)
        cond_1024 = 0.000887014 + 1.03683 * jax.random.normal(jax.random.fold_in(_rk, 11), (16, 512), jnp.float32)
        return (x, cond_1024)
    x, cond_1024 = _rec_inputs()

    def _L0_cond_setup():
        import math
        import jax, jax.numpy as jnp
        import numpy as np
        D_MODEL = 512
        N_HEADS = 16
        FFN_DIM = 2048
        EPS = 1e-05

        def _layernorm(x, w, b):
            mu = jnp.mean(x, axis=-1, keepdims=True)
            var = jnp.var(x, axis=-1, keepdims=True)
            return (x - mu) * jax.lax.rsqrt(var + EPS) * w + b

        def _modulate(x, shift, scale):
            return x * (1.0 + scale[:, None, :]) + shift[:, None, :]
        key = jax.random.key(seed)
        ks = jax.random.split(key, 16)
        B, S, D, F = (2, 1024, D_MODEL, FFN_DIM)
        s = 0.02
        return {'x': jax.random.normal(ks[0], (B, S, D), jnp.float32), 't_emb': jax.random.normal(ks[1], (B, D), jnp.float32), 'ln1_w': jnp.ones((D,), jnp.float32), 'ln1_b': jnp.zeros((D,), jnp.float32), 'ln2_w': jnp.ones((D,), jnp.float32), 'ln2_b': jnp.zeros((D,), jnp.float32), 'wq': jax.random.normal(ks[2], (D, D), jnp.float32) * s, 'bq': jnp.zeros((D,), jnp.float32), 'wk': jax.random.normal(ks[3], (D, D), jnp.float32) * s, 'bk': jnp.zeros((D,), jnp.float32), 'wv': jax.random.normal(ks[4], (D, D), jnp.float32) * s, 'bv': jnp.zeros((D,), jnp.float32), 'wo': jax.random.normal(ks[5], (D, D), jnp.float32) * s, 'bo': jnp.zeros((D,), jnp.float32), 'wt_attn': jax.random.normal(ks[6], (D, 2 * D), jnp.float32) * s, 'bt_attn': jnp.zeros((2 * D,), jnp.float32), 'wt_ffn': jax.random.normal(ks[7], (D, 2 * D), jnp.float32) * s, 'bt_ffn': jnp.zeros((2 * D,), jnp.float32), 'w1': jax.random.normal(ks[8], (D, F), jnp.float32) * s, 'b1': jnp.zeros((F,), jnp.float32), 'w2': jax.random.normal(ks[9], (F, D), jnp.float32) * s, 'b2': jnp.zeros((D,), jnp.float32)}
    _L0_cond_all = _L0_cond_setup()
    _L0_cond_in = {k: v for k, v in _L0_cond_all.items() if k in ('ln1_w', 'ln1_b', 'ln2_w', 'ln2_b', 'wq', 'bq', 'wk', 'bk', 'wv', 'bv', 'wo', 'bo', 'wt_attn', 'bt_attn', 'wt_ffn', 'bt_ffn', 'w1', 'b1', 'w2', 'b2')}
    del _L0_cond_all
    return {'x': x, 'cond_1024': cond_1024, 'L0_cond_ln1_w': _L0_cond_in['ln1_w'], 'L0_cond_ln1_b': _L0_cond_in['ln1_b'], 'L0_cond_ln2_w': _L0_cond_in['ln2_w'], 'L0_cond_ln2_b': _L0_cond_in['ln2_b'], 'L0_cond_wq': _L0_cond_in['wq'], 'L0_cond_bq': _L0_cond_in['bq'], 'L0_cond_wk': _L0_cond_in['wk'], 'L0_cond_bk': _L0_cond_in['bk'], 'L0_cond_wv': _L0_cond_in['wv'], 'L0_cond_bv': _L0_cond_in['bv'], 'L0_cond_wo': _L0_cond_in['wo'], 'L0_cond_bo': _L0_cond_in['bo'], 'L0_cond_wt_attn': _L0_cond_in['wt_attn'], 'L0_cond_bt_attn': _L0_cond_in['bt_attn'], 'L0_cond_wt_ffn': _L0_cond_in['wt_ffn'], 'L0_cond_bt_ffn': _L0_cond_in['bt_ffn'], 'L0_cond_w1': _L0_cond_in['w1'], 'L0_cond_b1': _L0_cond_in['b1'], 'L0_cond_w2': _L0_cond_in['w2'], 'L0_cond_b2': _L0_cond_in['b2']}

def reference(x, cond_1024, L0_cond_ln1_w, L0_cond_ln1_b, L0_cond_ln2_w, L0_cond_ln2_b, L0_cond_wq, L0_cond_bq, L0_cond_wk, L0_cond_bk, L0_cond_wv, L0_cond_bv, L0_cond_wo, L0_cond_bo, L0_cond_wt_attn, L0_cond_bt_attn, L0_cond_wt_ffn, L0_cond_bt_ffn, L0_cond_w1, L0_cond_b1, L0_cond_w2, L0_cond_b2):
    import jax
    import jax.numpy as jnp

    def _L0_cond_ref(x, t_emb, ln1_w, ln1_b, ln2_w, ln2_b, wq, bq, wk, bk, wv, bv, wo, bo, wt_attn, bt_attn, wt_ffn, bt_ffn, w1, b1, w2, b2):
        import math
        import jax, jax.numpy as jnp
        import numpy as np
        D_MODEL = 512
        N_HEADS = 16
        FFN_DIM = 2048
        EPS = 1e-05

        def _layernorm(x, w, b):
            mu = jnp.mean(x, axis=-1, keepdims=True)
            var = jnp.var(x, axis=-1, keepdims=True)
            return (x - mu) * jax.lax.rsqrt(var + EPS) * w + b

        def _modulate(x, shift, scale):
            return x * (1.0 + scale[:, None, :]) + shift[:, None, :]
        B, S, D = x.shape
        H = N_HEADS
        hd = D // H
        residual = x
        xn = _layernorm(x, ln1_w, ln1_b)
        t_attn = t_emb @ wt_attn + bt_attn
        shift_a, scale_a = jnp.split(t_attn, 2, axis=-1)
        xn = _modulate(xn, shift_a, scale_a)
        q = (xn @ wq + bq).reshape(B, S, H, hd).transpose(0, 2, 1, 3)
        k = (xn @ wk + bk).reshape(B, S, H, hd).transpose(0, 2, 1, 3)
        v = (xn @ wv + bv).reshape(B, S, H, hd).transpose(0, 2, 1, 3)
        scores = jnp.einsum('bhqd,bhkd->bhqk', q, k) / math.sqrt(hd)
        attn = jax.nn.softmax(scores, axis=-1)
        out = jnp.einsum('bhqk,bhkd->bhqd', attn, v)
        out = out.transpose(0, 2, 1, 3).reshape(B, S, D)
        x = residual + (out @ wo + bo)
        residual = x
        xn = _layernorm(x, ln2_w, ln2_b)
        t_ffn = t_emb @ wt_ffn + bt_ffn
        shift_f, scale_f = jnp.split(t_ffn, 2, axis=-1)
        xn = _modulate(xn, shift_f, scale_f)
        h = jax.nn.gelu(xn @ w1 + b1, approximate=False)
        x = residual + (h @ w2 + b2)
        return x
    x = _L0_cond_ref(x, cond_1024, L0_cond_ln1_w, L0_cond_ln1_b, L0_cond_ln2_w, L0_cond_ln2_b, L0_cond_wq, L0_cond_bq, L0_cond_wk, L0_cond_bk, L0_cond_wv, L0_cond_bv, L0_cond_wo, L0_cond_bo, L0_cond_wt_attn, L0_cond_bt_attn, L0_cond_wt_ffn, L0_cond_bt_ffn, L0_cond_w1, L0_cond_b1, L0_cond_w2, L0_cond_b2)
    return x

_drawn_inputs = setup_inputs


def setup_inputs(seed=0):
    import zlib

    import numpy as np

    out = dict(_drawn_inputs(seed))
    spreads = {'L0_cond_ln1_w': (1.0, 0.6),
     'L0_cond_ln1_b': (0.0, 0.338),
     'L0_cond_ln2_w': (1.0, 0.2),
     'L0_cond_ln2_b': (0.0, 0.315),
     'L0_cond_bq': (0.0, 0.8),
     'L0_cond_bk': (0.0, 0.8),
     'L0_cond_bv': (0.0, 0.1),
     'L0_cond_bo': (0.0, 0.1),
     'L0_cond_bt_attn': (0.0, 0.342),
     'L0_cond_bt_ffn': (0.0, 0.1),
     'L0_cond_b1': (0.0, 0.1),
     'L0_cond_b2': (0.0, 0.1)}
    factors = {'L0_cond_wq': 8.0, 'L0_cond_wk': 8.0}
    for name, (base, spread) in spreads.items():
        noise = np.random.default_rng([zlib.crc32(name.encode()), seed]).standard_normal(out[name].shape)
        drawn = base * np.exp(spread * noise) if base else spread * noise
        out[name] = jnp.asarray(drawn.astype(out[name].dtype))
    for name, factor in factors.items():
        out[name] = (out[name] * factor).astype(out[name].dtype)
    return out
```

```python
from contextlib import ExitStack

import concourse.bass as bass
from concourse import mybir

ALU = mybir.AluOpType
ACT = mybir.ActivationFunctionType
AX = mybir.AxisListType
F32 = mybir.dt.float32
F32R = mybir.dt.float32r

P = 128
HI, LO = 0, 1
PASSES = [(HI, HI), (HI, LO), (LO, HI)]
Q_LO, Q_HI, K_HI, K_LO = range(4)
STACK_PARTS = [slice(Q_HI, K_HI + 1), slice(Q_LO, K_HI + 1, 2), slice(Q_HI, K_LO + 1, 2)]
EPS = 1e-5
DMA = 16


def r(ap):
    return ap.bitcast(F32R)


def wait(eng, sem, value):
    if isinstance(value, int) and value <= 0:
        return
    eng.wait_ge(sem, value)


def waits(eng, met, *pairs):
    for _, value in pairs:
        if not isinstance(value, int):
            eng.compute_val(value)
    eng.wait_ge(met, 1)
    for sem, value in pairs:
        wait(eng, sem, value)


def conditioned_layer(nc, x, cond, ln1_w, ln1_b, ln2_w, ln2_b, wq, bq, wk, bk, wv, bv, wo, bo,
                      wt_attn, bt_attn, wt_ffn, bt_ffn, w1, b1, w2, b2, attn_out, out):
    NB, T, D = x.shape
    F = w1.shape[1]
    HD = 32
    NH = D // HD
    TT = T // P
    KD = D // P
    KF = F // P
    HG = P // HD
    NG = NH // HG
    RING = 8
    SUB = 4
    VW = 2 * HD + 1
    SCALE = float(HD) ** -0.5
    assert TT == SUB and KD == SUB and NG == SUB and NH == 16 and T == 512 and D == 512

    VECS = [("ln1_w", ln1_w), ("ln1_b", ln1_b), ("ln2_w", ln2_w), ("ln2_b", ln2_b), ("bq", bq), ("bk", bk),
            ("bv", bv), ("bt_attn", bt_attn), ("bt_ffn", bt_ffn), ("b1", b1)]
    col, n_vec = {}, 0
    for name, v in VECS:
        col[name] = n_vec
        n_vec += v.shape[0] // P

    x_v = x.rearrange("b (t p) d -> b p t d", p=P)
    y_v = attn_out.rearrange("b (t p) d -> b p t d", p=P)
    out_v = out.rearrange("b (t p) d -> b p t d", p=P)

    with ExitStack() as whole:
        def sb(ctx, name, shape):
            return ctx.enter_context(nc.sbuf_tensor(name, shape, F32))

        def sem(name):
            return whole.enter_context(nc.semaphore(name))

        ident = sb(whole, "ident", [P, P])
        vec = sb(whole, "vec", [P, n_vec])
        mod = sb(whole, "mod", [P, 2, 2, KD, NB])
        minus_half = sb(whole, "minus_half", [P, TT])
        stats = sb(whole, "stats", [P, TT, 6])
        mean_var = sb(whole, "mean_var", [P, TT, 2])
        neg_mean = sb(whole, "neg_mean", [P, TT])
        var_eps = sb(whole, "var_eps", [P, TT])
        rstd = sb(whole, "rstd", [P, TT])
        ps = [whole.enter_context(nc.psum_tensor(f"ps{i}", [P, 512], F32)) for i in range(8)]

        part1 = ExitStack()
        w_at = {n: sb(part1, f"w_{n}", [P, 2, KD, D]) for n in ("q", "k", "v", "o")}

        scratch = ExitStack()
        vec_rows = sb(scratch, "vec_rows", [n_vec, P])
        cond_rows = sb(scratch, "cond_rows", [NB, D])
        condT = sb(scratch, "condT", [P, KD, NB])
        one_plus = sb(scratch, "one_plus", [P, NB])
        shift_part = sb(scratch, "shift_part", [P, NB])
        wt_raw = [sb(scratch, f"wt_raw{i}", [P, KD, 2 * D]) for i in range(2)]
        w_raw = {n: sb(scratch, f"w_raw_{n}", [P, KD, D]) for n in w_at}

        vec_landed, cond_landed, wt_landed = sem("vec_landed"), sem("cond_landed"), sem("wt_landed")
        w_landed = {n: sem(f"w_landed_{n}") for n in w_at}
        ident_zero, ident_done, half_done = sem("ident_zero"), sem("ident_done"), sem("half_done")
        vec_turned, vec_done, cond_turned, condT_done = sem("vec_turned"), sem("vec_done"), sem("cond_turned"), sem("condT_done")
        mod_ready, mod_step, w_hi_done, w_lo_done = sem("mod_ready"), sem("mod_step"), sem("w_hi_done"), sem("w_lo_done")

        with nc.Block() as block:
            @block.sync
            def _(sp):
                for name, v in VECS:
                    n = v.shape[0] // P
                    sp.dma_start(vec_rows[col[name]:col[name] + n, :],
                                 v.rearrange("(r c) -> r c", c=P)).then_inc(vec_landed, DMA)
                sp.dma_start(cond_rows[:], cond).then_inc(cond_landed, DMA)
                for n, w in (("k", wk), ("q", wq), ("v", wv), ("o", wo)):
                    sp.dma_start(w_raw[n][:], w.rearrange("(k p) n -> p k n", p=P)).then_inc(w_landed[n], DMA)
                sp.wait_ge(w_lo_done, 4)

            @block.gpsimd
            def _(pool):
                pool.memset(ident[:], 0.0).then_inc(ident_zero, 1)
                pool.wait_ge(ident_zero, 1)
                pool.affine_select(out=ident[:], in_=ident[:], compare_op=ALU.not_equal, fill=1.0, base=0,
                                   pattern=[[-1, P]], channel_multiplier=1).then_inc(ident_done, 1)
                pool.memset(minus_half[:], -0.5).then_inc(half_done, 1)
                pool.wait_ge(half_done, 1)

            @block.tensor
            def _(pe):
                pe.wait_ge(ident_done, 1)
                pe.wait_ge(vec_landed, DMA * len(VECS))
                pe.transpose(ps[0][:, 0:n_vec], vec_rows[:], ident[0:n_vec, 0:n_vec]).then_inc(vec_turned, 1)
                pe.wait_ge(cond_landed, DMA)
                for k in range(KD):
                    last = pe.transpose(ps[1][:, k * NB:(k + 1) * NB], cond_rows[:, k * P:(k + 1) * P],
                                        ident[0:NB, 0:NB])
                last.then_inc(cond_turned, 1)
                pe.wait_ge(condT_done, 1)
                pe.wait_ge(wt_landed, 2 * DMA)
                for i in range(2):
                    for m in range(2 * KD):
                        for k in range(KD):
                            last = pe.matmul(ps[2][:, (8 * i + m) * NB:(8 * i + m + 1) * NB],
                                             wt_raw[i][:, k, m * P:(m + 1) * P], condT[:, k, :],
                                             start=(k == 0), stop=(k == KD - 1))
                last.then_inc(mod_ready, 1)

            @block.scalar
            def _(act):
                for i, w in enumerate((wt_attn, wt_ffn)):
                    act.dma_start(wt_raw[i][:], w.rearrange("(k p) n -> p k n", p=P)).then_inc(wt_landed, DMA)
                for n in ("k", "q", "v", "o"):
                    act.wait_ge(w_landed[n], DMA)
                    act.activation(r(w_at[n][:, HI]), w_raw[n][:], ACT.Copy).then_inc(w_hi_done, 1)

            @block.vector
            def _(dve):
                dve.wait_ge(vec_turned, 1)
                dve.tensor_copy(vec[:], ps[0][:, 0:n_vec]).then_inc(vec_done, 1)
                dve.wait_ge(cond_turned, 1)
                dve.tensor_copy(condT[:].rearrange("p k b -> p (k b)"), ps[1][:, 0:KD * NB]).then_inc(condT_done, 1)
                for i, n in enumerate(("k", "q", "v", "o")):
                    dve.wait_ge(w_hi_done, i + 1)
                    dve.tensor_tensor(r(w_at[n][:, LO]), w_raw[n][:], w_at[n][:, HI], ALU.subtract).then_inc(w_lo_done, 1)
                dve.wait_ge(mod_ready, 1)
                dve.wait_ge(vec_done, 1)
                step = 0
                for i, (w_c, b_c, t_c) in enumerate(((col["ln1_w"], col["ln1_b"], col["bt_attn"]),
                                                    (col["ln2_w"], col["ln2_b"], col["bt_ffn"]))):
                    for f in range(KD):
                        shift_ps = ps[2][:, (8 * i + f) * NB:(8 * i + f + 1) * NB]
                        scale_ps = ps[2][:, (8 * i + KD + f) * NB:(8 * i + KD + f + 1) * NB]
                        dve.tensor_scalar(one_plus[:], scale_ps, vec[:, t_c + KD + f:t_c + KD + f + 1], 1.0,
                                          ALU.add, ALU.add).then_inc(mod_step, 1)
                        dve.wait_ge(mod_step, step + 1)
                        dve.tensor_scalar(mod[:, i, 0, f, :], one_plus[:], vec[:, w_c + f:w_c + f + 1], None,
                                          ALU.mult).then_inc(mod_step, 1)
                        dve.tensor_scalar(shift_part[:], one_plus[:], vec[:, b_c + f:b_c + f + 1],
                                          vec[:, t_c + f:t_c + f + 1], ALU.mult, ALU.add).then_inc(mod_step, 1)
                        dve.wait_ge(mod_step, step + 3)
                        dve.tensor_tensor(mod[:, i, 1, f, :], shift_part[:], shift_ps, ALU.add).then_inc(mod_step, 1)
                        step += 4
                        dve.wait_ge(mod_step, step)

        scratch.close()

        stack = sb(part1, "stack", [P, RING, 2, T])
        v_op = sb(part1, "v_op", [P, TT, NH, VW])
        p_full = sb(part1, "p_full", [P, 2, T])
        p_hi = sb(part1, "p_hi", [P, 4, T])
        p_lo = sb(part1, "p_lo", [P, 4, T])
        xnT = sb(part1, "xnT", [P, 2, KD, T])
        staging = sb(part1, "staging", [P, 4, T])
        u_sb = sb(part1, "u_sb", [VW, 2, T])
        halves = sb(part1, "halves", [P, 2, 2, T])
        recip_b = sb(part1, "recip_b", [P, T])
        rows = sb(part1, "rows", [P, T])
        sums = sb(part1, "sums", [HG * 16, T // 16])
        recips = sb(part1, "recips", [HG * 16, T // 16])
        attnT = sb(part1, "attnT", [P, 2, NG, T])
        xz = sb(part1, "xz", [P, TT, D])
        xt = sb(part1, "xt", [P, T])
        y_sb = sb(part1, "y_sb", [P, 2, D])
        neg_max = sb(part1, "neg_max", [P, 2, TT, 2])

        ST, S, G, TR, U = ps[0:2], ps[2:4], ps[4:6], ps[6], ps[7]

        def whole_slot(t):
            return [SUB * t + s for s in range(SUB)]
        UNITS = [("k", 0, 2, whole_slot(0)), ("q", 0, 2, whole_slot(1)), ("v", 0, 2, whole_slot(2)),
                 ("v", 0, 3, whole_slot(3)), ("k", 0, 3, whole_slot(4)), ("q", 0, 3, whole_slot(5)),
                 ("o", -1, 0, [24, 25, 26]), ("o", -1, 1, [27, 28, 29]), ("o", -1, 2, [30, 31, 32]),
                 ("o", -1, 3, [33, 34, 35]), ("k", 1, 0, whole_slot(9)), ("q", 1, 0, whole_slot(10)),
                 ("v", 1, 0, whole_slot(11)), ("k", 1, 1, whole_slot(12)), ("q", 1, 1, whole_slot(13)),
                 ("v", 1, 1, [56, 58, 60, 61])]
        EVACUATED_AT = {i: subs[-1] + 1 for i, (_, _, _, subs) in enumerate(UNITS)}
        EVACUATED_AT[13] = 53
        TURNS = sorted([(SUB * t + 1, "neg", (t + 2) // NH, (t + 2) % NH // 2) for t in range(0, NH, 2)]
                       + [(27, "x", 1, 0), (29, "x", 1, 1), (31, "x", 1, 2), (35, "x", 1, 3)])
        X_COPY_AT = {28: 0, 30: 1, 32: 2, 36: 3}
        ATTN_AT = {37: (0, 0), 49: (0, 1), 1: (-1, 2), 17: (-1, 3)}
        RECIP_AT = {23: (0, 0), 39: (0, 1), 55: (0, 2), 7: (-1, 3)}
        STACK_AT = {0: [(0, 7)], 10: [(0, 8)], 11: [(0, 9)], 13: [(0, 10)], 16: [(0, 11)],
                    26: [(0, 12)], 27: [(0, 13)], 29: [(0, 14)], 32: [(0, 15)],
                    45: [(1, 0)], 47: [(1, 1)], 48: [(1, 2)], 49: [(1, 3)],
                    57: [(1, 4)], 58: [(1, 5)], 60: [(1, 6)]}

        st_ready, exp_done, split_done, av_done = sem("st_ready"), sem("exp_done"), sem("split_done"), sem("av_done")
        s_ready, max_done = sem("s_ready"), sem("max_done")
        neg_turned, neg_copied = sem("neg_turned"), sem("neg_copied")
        neg_landed = [sem(f"neg_landed{i}") for i in range(2)]
        u_copied, halves_added, normed = sem("u_copied"), sem("halves_added"), sem("normed")
        halves_landed = [sem(f"halves_landed{i}") for i in range(2)]
        sum_landed = [sem(f"sum_landed{i}") for i in range(2)]
        recip_done, recip_row_landed, recip_b_landed = sem("recip_done"), sem("recip_row_landed"), sem("recip_b_landed")
        attn_hi, attn_lo = sem("attn_hi"), sem("attn_lo")
        x_landed, stats_done, mv_done = sem("x_landed"), sem("stats_done"), sem("mv_done")
        moments_done, rstd_done, z_done = sem("moments_done"), sem("rstd_done"), sem("z_done")
        x_turned, xt_copied, xn_hi, xn_lo = sem("x_turned"), sem("xt_copied"), sem("xn_hi"), sem("xn_lo")
        qk_ready, qk_hi, qk_lo = sem("qk_ready"), sem("qk_hi"), sem("qk_lo")
        stack_landed = [sem(f"stack_landed{i}") for i in range(RING)]
        v_ready, v_hi, v_lo = sem("v_ready"), sem("v_hi"), sem("v_lo")
        o_ready, y_copied = sem("o_ready"), sem("y_copied")
        y_stored = [sem(f"y_stored{i}") for i in range(2)]

        def unit_index(kind, b, n):
            if kind in "qk":
                return 2 * KD * b + 2 * n + (kind == "q")
            return 4 * b + n

        def unit_exists(live, i):
            return UNITS[i][1] in live

        def bank_freed(b, live, i):
            freed = {"k": qk_lo, "q": qk_lo, "v": v_lo, "o": y_copied}
            j, back = i - 2, 0
            while True:
                if j < 0:
                    j, back = j + len(UNITS), back + 1
                kind, rel, n, _ = UNITS[j]
                if isinstance(b, int):
                    if b - back < -1:
                        return freed[kind], 0
                    if not 0 <= b - back + rel < NB:
                        j -= 2
                        continue
                return freed[kind], unit_index(kind, b - back + rel, n) + 1

        def turn_bank_freed(b, i):
            freed = {"neg": neg_copied, "x": xt_copied}
            j, back = i - 1, 0
            while True:
                if j < 0:
                    j, back = j + len(TURNS), back + 1
                _, kind, rel, n = TURNS[j]
                if isinstance(b, int):
                    if b - back < -1:
                        return freed[kind], 0
                    if not 0 <= b - back + rel < NB:
                        j -= 1
                        continue
                return freed[kind], (8 if kind == "neg" else KD) * (b - back + rel) + n + 1

        def passes(eng, one_pass):
            one_pass(-1, {1})
            one_pass(0, {0, 1})
            one_pass(1, {-1, 0, 1})
            with eng.Fori(2, NB - 1) as b:
                one_pass(b, {-1, 0, 1})
            one_pass(NB - 1, {-1, 0})
            one_pass(NB, {-1})

        def lagging(tau, lag):
            u = tau - lag
            return (0 if u >= 0 else -1), (u % 64) // SUB, u % SUB

        ones_done = sem("ones_done")

        with nc.Block() as block:
            @block.tensor
            def _(pe):
                pe.wait_ge(ones_done, 2)

                def project(b, i, part):
                    kind, rel, n, subs = UNITS[i]
                    bank, bb = G[i % 2], b + rel
                    if part == 0:
                        wait(pe, *bank_freed(b, None, i))
                    if kind in "qk":
                        if kind == "k" and n == 0:
                            wait(pe, xn_lo, KD * bb + part + 1)
                        for j, (a, c) in enumerate(PASSES):
                            last = pe.matmul(bank[:], r(w_at[kind][:, a, part, n * P:(n + 1) * P]),
                                             r(xnT[:, c, part, :]), start=(part == 0 and j == 0),
                                             stop=(part == KD - 1 and j == 2))
                        if part == KD - 1:
                            last.then_inc(qk_ready, 1)
                    elif kind == "v":
                        half, tile = n // 2, 2 * (n % 2) + part // 2
                        o = bank[:, (part // 2) * 256:(part // 2) * 256 + 256]
                        for k in (2 * (part % 2), 2 * (part % 2) + 1):
                            for j, (a, c) in enumerate(PASSES):
                                last = pe.matmul(o, r(xnT[:, a, k, tile * P:(tile + 1) * P]),
                                                 r(w_at["v"][:, c, k, half * 256:half * 256 + 256]),
                                                 start=(k == 0 and j == 0), stop=(k == KD - 1 and j == 2))
                        if part == 3:
                            last.then_inc(v_ready, 1)
                    else:
                        for m in range(4 * part, 4 * part + 4):
                            g, j = m // 3, m % 3
                            a, c = PASSES[j]
                            if n == 0 and j == 0:
                                wait(pe, attn_lo, NG * bb + g + 1)
                            last = pe.matmul(bank[:], r(attnT[:, a, g, n * P:(n + 1) * P]),
                                             r(w_at["o"][:, c, g, :]), start=(m == 0), stop=(m == 11))
                        if part == 2:
                            last.then_inc(o_ready, 1)

                def attend(b, live, tau):
                    rel, h, kt = lagging(tau, 3)
                    if rel in live:
                        n = 64 * (b + rel) + SUB * h + kt
                        wait(pe, split_done, n + 1)
                        if kt == 0:
                            wait(pe, u_copied, NH * (b + rel) + h)
                        if kt == 0 and h % 8 == 0:
                            wait(pe, v_lo, 4 * (b + rel) + 2 + h // 4)
                        pe.matmul(U[0:VW, :], r(v_op[:, kt, h, :]), r(p_hi[:, kt, :]),
                                  start=(kt == 0), stop=False)
                        pe.matmul(U[0:VW, :], r(v_op[:, kt, h, :]), r(p_lo[:, kt, :]),
                                  start=False, stop=(kt == TT - 1)).then_inc(av_done, 1)

                def one_pass(b, live):
                    for tau in range(64):
                        t, s = tau // SUB, tau % SUB
                        if 0 in live:
                            n = 64 * b + tau
                            wait(pe, exp_done, n - 1)
                            if s == 0 and t % 2 == 0:
                                wait(pe, neg_landed[t // 2 % 2], DMA * (4 * b + t // 4 + 1))
                            pe.matmul(ST[tau % 2][:], r(stack[0:97, t % RING, 1, s * P:(s + 1) * P]),
                                      r(stack[0:97, t % RING, 0, :]), start=True, stop=True).then_inc(st_ready, 1)
                        rel, h = (t + 4) // NH, (t + 4) % NH
                        if rel in live:
                            m = 64 * (b + rel) + SUB * h + s
                            wait(pe, max_done, m - 1)
                            if s == 0:
                                wait(pe, stack_landed[h % RING], 3 * DMA * (2 * (b + rel) + h // RING + 1))
                            pe.matmul(S[tau % 2][:], r(stack[0:96, h % RING, 0, s * P:(s + 1) * P]),
                                      r(stack[0:96, h % RING, 1, :]), start=True, stop=True).then_inc(s_ready, 1)
                        if s == 2:
                            attend(b, live, tau)
                        for i, (_, rel, _, subs) in enumerate(UNITS):
                            if tau in subs and rel in live:
                                project(b, i, subs.index(tau))
                        for i, (at, kind, rel, n) in enumerate(TURNS):
                            if at != tau or rel not in live:
                                continue
                            if kind == "neg":
                                wait(pe, max_done, 64 * (b + rel) + 8 * n + 8)
                                wait(pe, *turn_bank_freed(b, i))
                                for q in range(TT):
                                    last = pe.transpose(TR[0:2, q * P:(q + 1) * P], neg_max[:, n % 2, q, :], ident[:])
                                last.then_inc(neg_turned, 1)
                            else:
                                wait(pe, z_done, TT * (b + rel + 1))
                                wait(pe, *turn_bank_freed(b, i))
                                for q in range(TT):
                                    last = pe.transpose(TR[:, q * P:(q + 1) * P], xz[:, q, n * P:(n + 1) * P], ident[:])
                                last.then_inc(x_turned, 1)
                        if s != 2:
                            attend(b, live, tau)

                passes(pe, one_pass)

            @block.scalar
            def _(act):
                def evacuate(b, i):
                    kind, rel, n, _ = UNITS[i]
                    bank, bb = G[i % 2], b + rel
                    if kind in "qk":
                        wait(act, qk_ready, unit_index(kind, bb, n) + 1)
                        if kind == "k":
                            for j in range(HG):
                                wait(act, stack_landed[(n + 1) % 2 * HG + j], 3 * DMA * (2 * bb + (n + 1) // 2))
                        part, bias = (K_HI, col["bk"]) if kind == "k" else (Q_HI, col["bq"])
                        act.activation(r(staging[:, part, :]), bank[:], ACT.Identity,
                                       bias=vec[:, bias + n:bias + n + 1]).then_inc(qk_hi, 1)
                    elif kind == "v":
                        wait(act, v_ready, 4 * bb + n + 1)
                        wait(act, av_done, 64 * bb - 32 if n < 2 else 64 * bb)
                        k, h = 2 * (n % 2), 8 * (n // 2)
                        act.activation(r(v_op[:, k:k + 2, h:h + 8, 0:HD]),
                                       bank[:].rearrange("p (k h e) -> p k h e", k=2, h=8), ACT.Copy).then_inc(v_hi, 1)
                    else:
                        wait(act, o_ready, 4 * bb + n + 1)
                        wait(act, y_stored[n % 2], DMA * (2 * bb + n // 2))
                        act.activation(y_sb[:, n % 2, :], bank[:], ACT.Copy).then_inc(y_copied, 1)

                def one_pass(b, live):
                    for tau in range(64):
                        t, s = tau // SUB, tau % SUB
                        if 0 in live:
                            n = 64 * b + tau
                            wait(act, st_ready, n + 1)
                            wait(act, av_done, n - 3)
                            act.activation(r(p_hi[:, tau % 4, :]), ST[tau % 2][:], ACT.Exp, scale=SCALE)
                        if s == 2:
                            rel, h = (0, t - 1) if t >= 1 else (-1, NH - 1)
                            if rel in live:
                                bb = b + rel
                                wait(act, av_done, 64 * bb + SUB * h + 4)
                                wait(act, halves_landed[h % 2], 2 * DMA * (8 * bb + h // 2))
                                wait(act, sum_landed[h % 2], DMA * (8 * bb + h // 2))
                                act.activation(u_sb[:, h % 2, :], U[0:VW, :], ACT.Copy).then_inc(u_copied, 1)
                        if 0 in live:
                            wait(act, split_done, n - 1)
                            act.activation(p_full[:, tau % 2, :], ST[tau % 2][:], ACT.Exp,
                                           scale=SCALE).then_inc(exp_done, 1)
                        for at, kind, rel, n in TURNS:
                            if kind == "neg" and at + 1 == tau and rel in live:
                                bb = b + rel
                                wait(act, neg_turned, 8 * bb + n + 1)
                                wait(act, neg_landed[n % 2], DMA * (4 * bb + n // 2))
                                p0 = 64 * (n % 2)
                                act.activation(r(rows[p0:p0 + 2, :]), TR[0:2, :], ACT.Copy).then_inc(neg_copied, 1)
                        if tau in X_COPY_AT and 1 in live:
                            f, bb = X_COPY_AT[tau], b + 1
                            wait(act, x_turned, KD * bb + f + 1)
                            wait(act, xn_lo, KD * bb + f)
                            act.activation(xt[:], TR[:], ACT.Identity, bias=mod[:, 0, 1, f, bass.ds(bb, 1)],
                                           scale=mod[:, 0, 0, f, bass.ds(bb, 1)]).then_inc(xt_copied, 1)
                        for i, (_, rel, _, _) in enumerate(UNITS):
                            if EVACUATED_AT[i] == tau and rel in live:
                                evacuate(b, i)
                        if tau in ATTN_AT and ATTN_AT[tau][0] in live:
                            rel, g = ATTN_AT[tau]
                            bb = b + rel
                            wait(act, normed, NG * bb + g + 1)
                            wait(act, o_ready, 4 * bb)
                            act.activation(r(attnT[:, HI, g, :]), halves[:, g % 2, 0, :], ACT.Identity,
                                           bias=vec[:, col["bv"] + g:col["bv"] + g + 1]).then_inc(attn_hi, 1)

                passes(act, one_pass)

            @block.vector
            def _(dve):
                dve.memset(v_op[:, :, :, 2 * HD:VW], 1.0).then_inc(ones_done, 1)
                dve.memset(stack[96:97, :, 1, :], 1.0).then_inc(ones_done, 1)

                def evacuate(b, i):
                    kind, rel, n, _ = UNITS[i]
                    bank, bb = G[i % 2], b + rel
                    if kind in "qk":
                        wait(dve, qk_hi, unit_index(kind, bb, n) + 1)
                        hi, lo, bias = (K_HI, K_LO, col["bk"]) if kind == "k" else (Q_HI, Q_LO, col["bq"])
                        dve.scalar_tensor_tensor(r(staging[:, lo, :]), bank[:], vec[:, bias + n:bias + n + 1],
                                                 staging[:, hi, :], ALU.add, ALU.subtract).then_inc(qk_lo, 1)
                    elif kind == "v":
                        wait(dve, v_hi, 4 * bb + n + 1)
                        k, h = 2 * (n % 2), 8 * (n // 2)
                        dve.tensor_tensor(r(v_op[:, k:k + 2, h:h + 8, HD:2 * HD]),
                                          bank[:].rearrange("p (k h e) -> p k h e", k=2, h=8),
                                          v_op[:, k:k + 2, h:h + 8, 0:HD], ALU.subtract).then_inc(v_lo, 1)

                def one_pass(b, live):
                    for tau in range(64):
                        t, s = tau // SUB, tau % SUB
                        for i, (_, rel, _, _) in enumerate(UNITS):
                            if EVACUATED_AT[i] + 1 == tau and rel in live:
                                evacuate(b, i)
                        rel, h = (t + 4) // NH, (t + 4) % NH
                        if rel in live:
                            bb = b + rel
                            wait(dve, s_ready, 64 * bb + SUB * h + s + 1)
                            if s == 0 and h % 2 == 0:
                                wait(dve, neg_turned, 8 * bb + h // 2 - 1)
                            dve.tensor_reduce(neg_max[:, h // 2 % 2, s, h % 2:h % 2 + 1], S[tau % 2][:], AX.X,
                                              ALU.max, negate=True).then_inc(max_done, 1)
                        rel, h, kt = lagging(tau, 1)
                        if rel in live:
                            n = 64 * (b + rel) + SUB * h + kt
                            wait(dve, exp_done, n + 1)
                            dve.tensor_tensor(r(p_lo[:, kt, :]), p_full[:, kt % 2, :], p_hi[:, kt, :],
                                              ALU.subtract).then_inc(split_done, 1)
                        if 1 in live and tau in (8, 10, 12, 14):
                            i = (tau - 8) // 2
                            wait(dve, x_landed, DMA * (b + 2))
                            wait(dve, mv_done, TT * (b + 1))
                            dve.bn_stats(stats[:, i, :], xz[:, i, :]).then_inc(stats_done, 1)
                        if 1 in live and tau in (9, 11, 13, 15):
                            i = (tau - 9) // 2
                            waits(dve, half_done, (stats_done, TT * (b + 1) + i + 1),
                                  (z_done, TT * (b + 1)))
                            dve.bn_aggr(mean_var[:, i, :], stats[:, i, :]).then_inc(mv_done, 1)
                        if tau - 1 in X_COPY_AT and 1 in live:
                            f, bb = X_COPY_AT[tau - 1], b + 1
                            if f == 0:
                                wait(dve, qk_ready, 2 * KD * bb)
                                wait(dve, v_ready, 4 * bb)
                            wait(dve, xt_copied, KD * bb + f + 1)
                            dve.tensor_copy(r(xnT[:, HI, f, :]), xt[:]).then_inc(xn_hi, 1)
                            wait(dve, xn_hi, KD * bb + f + 1)
                            dve.tensor_tensor(r(xnT[:, LO, f, :]), xt[:], xnT[:, HI, f, :],
                                              ALU.subtract).then_inc(xn_lo, 1)
                        if tau in RECIP_AT and RECIP_AT[tau][0] in live:
                            rel, g = RECIP_AT[tau]
                            bb = b + rel
                            for i in range(2):
                                wait(dve, sum_landed[i], DMA * (8 * bb + 2 * g + 2))
                            wait(dve, recip_row_landed, DMA * (NG * bb + g))
                            dve.reciprocal(recips[:], sums[:]).then_inc(recip_done, 1)
                        if tau - 1 in ATTN_AT and ATTN_AT[tau - 1][0] in live:
                            rel, g = ATTN_AT[tau - 1]
                            bb = b + rel
                            wait(dve, attn_hi, NG * bb + g + 1)
                            dve.scalar_tensor_tensor(r(attnT[:, LO, g, :]), halves[:, g % 2, 0, :],
                                                     vec[:, col["bv"] + g:col["bv"] + g + 1], attnT[:, HI, g, :],
                                                     ALU.add, ALU.subtract).then_inc(attn_lo, 1)

                passes(dve, one_pass)

            @block.gpsimd
            def _(pool):
                def normalise(bb, g):
                    waits(pool, half_done, (recip_done, NG * bb + g + 1))
                    pool.dma_start(rows[32:32 + HG, :], recips[:]).then_inc(recip_row_landed, DMA)
                    waits(pool, half_done, (recip_row_landed, DMA * (NG * bb + g + 1)))
                    for j in range(HG):
                        pool.dma_start(recip_b[HD * j:HD * (j + 1), :],
                                       rows[32 + j:33 + j, :].unsqueeze(1).broadcast_to([1, HD, T])
                                       ).then_inc(recip_b_landed, DMA)
                    for i in range(2):
                        wait(pool, halves_landed[i], 2 * DMA * (8 * bb + 2 * g + 2))
                    a = halves[:, g % 2, 0, :]
                    pool.tensor_tensor(a, a, halves[:, g % 2, 1, :], ALU.add).then_inc(halves_added, 1)
                    wait(pool, halves_added, NG * bb + g + 1)
                    wait(pool, recip_b_landed, HG * DMA * (NG * bb + g + 1))
                    pool.tensor_tensor(a, a, recip_b[:], ALU.mult).then_inc(normed, 1)

                def one_pass(b, live):
                    if -1 in live:
                        normalise(b - 1, 3)
                    if 1 in live:
                        bb = b + 1
                        waits(pool, half_done, (mv_done, TT * (bb + 1)))
                        pool.tensor_scalar(neg_mean[:], mean_var[:, :, 0], -1.0, 0.0, ALU.mult, ALU.add).then_inc(moments_done, 1)
                        pool.tensor_scalar(var_eps[:], mean_var[:, :, 1], EPS, 1.0, ALU.add, ALU.mult).then_inc(moments_done, 1)
                        wait(pool, moments_done, 2 * (bb + 1))
                        pool.tensor_tensor(rstd[:], var_eps[:], minus_half[:], ALU.pow).then_inc(rstd_done, 1)
                        waits(pool, half_done, (rstd_done, bb + 1))
                        for i in range(TT):
                            pool.tensor_scalar(xz[:, i, :], xz[:, i, :], neg_mean[:, i:i + 1], rstd[:, i:i + 1],
                                               ALU.add, ALU.mult).then_inc(z_done, 1)
                    if 0 in live:
                        for g in range(3):
                            normalise(b, g)

                passes(pool, one_pass)

            @block.sync
            def _(sp):
                def one_pass(b, live):
                    for tau in range(64):
                        t, s = tau // SUB, tau % SUB
                        if tau == 0 and 1 in live:
                            waits(sp, half_done, (x_turned, KD * (b + 1)))
                            sp.dma_start(xz[:], x_v[bass.ds(b + 1, 1)].rearrange("o p t d -> (o p) t d")
                                         ).then_inc(x_landed, DMA)
                        for rel, h in STACK_AT.get(tau, ()):
                            if rel not in live:
                                continue
                            bb, g, j = b + rel, h // HG, h % HG
                            waits(sp, half_done, (qk_lo, 2 * KD * bb + 2 * g + 2),
                                  (st_ready, 64 * bb + SUB * (h - RING) + 4))
                            for i, parts in enumerate(STACK_PARTS):
                                sp.dma_start(stack[HD * i:HD * (i + 1), h % RING, :, :],
                                             staging[HD * j:HD * (j + 1), parts, :]).then_inc(stack_landed[h % RING], DMA)
                        if s == 0:
                            rel, h = (0, t - 2) if t >= 2 else (-1, t + NH - 2)
                            if rel in live:
                                bb, j = b + rel, h % HG
                                waits(sp, half_done, (u_copied, NH * bb + h + 1),
                                      (recip_done, NG * bb + h // HG))
                                sp.dma_start(sums[16 * j:16 * j + 16, :], u_sb[2 * HD:VW, h % 2, :]
                                             ).then_inc(sum_landed[h % 2], DMA)
                                g = h // HG
                                if j == 0:
                                    waits(sp, half_done, (attn_lo, NG * bb + g - 1))
                                for c in range(2):
                                    sp.dma_start(halves[HD * j:HD * (j + 1), g % 2, c, :],
                                                 u_sb[HD * c:HD * (c + 1), h % 2, :]).then_inc(halves_landed[h % 2], DMA)
                        for at, kind, rel, n in TURNS:
                            if kind == "neg" and at + 2 == tau and rel in live:
                                bb, p0 = b + rel, 64 * (n % 2)
                                wait(sp, neg_copied, 8 * bb + n + 1)
                                h = 2 * n % RING
                                sp.dma_start(stack[96:97, h:h + 2, 0, :], rows[p0:p0 + 2, :]
                                             ).then_inc(neg_landed[n % 2], DMA)
                        for i, (kind, rel, n, _) in enumerate(UNITS):
                            if kind == "o" and EVACUATED_AT[i] + 1 == tau and rel in live:
                                bb = b + rel
                                waits(sp, half_done, (y_copied, 4 * bb + n + 1))
                                sp.dma_start(y_v[bass.ds(bb, 1), :, n, :].rearrange("o p d -> (o p) d"),
                                             y_sb[:, n % 2, :]).then_inc(y_stored[n % 2], DMA)

                passes(sp, one_pass)
                for i in range(2):
                    sp.wait_ge(y_stored[i], DMA * 2 * NB)
        part1.close()

        part2 = ExitStack()
        w1_sb = sb(part2, "w1_sb", [P, 2, KD, F])
        w2_sb = sb(part2, "w2_sb", [P, 2, KF, D])
        fw_landed = [sem(f"fw_landed{i}") for i in range(2)]
        fw_hi, fw_lo, bias_landed = sem("fw_hi"), sem("fw_lo"), sem("bias_landed")
        scratch = ExitStack()
        raw = [sb(scratch, f"ffn_raw{i}", [P, KD * F // 2]) for i in range(2)]
        w1_v = w1.rearrange("(k p) n -> p k n", p=P)
        w2_v = w2.rearrange("(k p) n -> p k n", p=P)
        PIECES = []
        for i in range(2):
            PIECES.append((w1_v[:, :, i * (F // 2):(i + 1) * (F // 2)],
                           [w1_sb[:, a, :, i * (F // 2):(i + 1) * (F // 2)] for a in (HI, LO)],
                           lambda ap: ap.rearrange("p (k n) -> p k n", k=KD)))
        for i in range(2):
            PIECES.append((w2_v[:, i * (KF // 2):(i + 1) * (KF // 2), :],
                           [w2_sb[:, a, i * (KF // 2):(i + 1) * (KF // 2), :] for a in (HI, LO)],
                           lambda ap: ap.rearrange("p (k n) -> p k n", k=KF // 2)))

        with nc.Block() as block:
            @block.sync
            def _(sp):
                for i, (src, _, shape) in enumerate(PIECES):
                    wait(sp, fw_lo, i - 1)
                    sp.dma_start(shape(raw[i % 2][:]), src).then_inc(fw_landed[i % 2], DMA)
            @block.scalar
            def _(act):
                for i, (_, dst, shape) in enumerate(PIECES):
                    act.wait_ge(fw_landed[i % 2], DMA * (i // 2 + 1))
                    act.activation(r(dst[HI]), shape(raw[i % 2][:]), ACT.Copy).then_inc(fw_hi, 1)

            @block.vector
            def _(dve):
                for i, (_, dst, shape) in enumerate(PIECES):
                    dve.wait_ge(fw_hi, i + 1)
                    dve.tensor_tensor(r(dst[LO]), shape(raw[i % 2][:]), dst[HI], ALU.subtract).then_inc(fw_lo, 1)
                dve.wait_ge(fw_lo, len(PIECES))

        scratch.close()

        fnT = sb(part2, "fnT", [P, 2, 2, KD, T])
        hid = sb(part2, "hid", [P, 2, 2, T])
        hid_full = sb(part2, "hid_full", [P, 2, T])
        res = sb(part2, "res", [P, 2, TT, D])
        yz = sb(part2, "yz", [P, TT, D])
        ft = sb(part2, "ft", [P, T])
        bo_b = sb(part2, "bo_b", [P, D])
        b2_b = sb(part2, "b2_b", [P, D])
        ACC, HB, TB = ps[0:4], ps[4:6], ps[6:8]
        TURN_AT = {8: 0, 9: 1, 10: 2, 11: 3}

        in_landed, out_stored = [sem(f"in_landed{i}") for i in range(2)], [sem(f"out_stored{i}") for i in range(2)]
        summed, res_done, fstats_done, fmv_done = sem("summed"), sem("res_done"), sem("fstats_done"), sem("fmv_done")
        fmoments_done, frstd_done, fz_done, b2_added = sem("fmoments_done"), sem("frstd_done"), sem("fz_done"), sem("b2_added")
        f_turned, ft_copied, fn_hi, fn_lo = sem("f_turned"), sem("ft_copied"), sem("fn_hi"), sem("fn_lo")
        h_ready, gelu_done, hid_hi, hid_lo = sem("h_ready"), sem("gelu_done"), sem("hid_hi"), sem("hid_lo")
        down_done, acc_read = sem("down_done"), sem("acc_read")

        def ffn_passes(eng, one_pass):
            one_pass(-1, 1, {1})
            one_pass(0, 0, {0, 1})
            one_pass(1, 1, {-1, 0, 1})
            with eng.Fori(2, NB - 2, 2) as b:
                one_pass(b, 0, {-1, 0, 1})
                one_pass(b + 1, 1, {-1, 0, 1})
            one_pass(NB - 2, 0, {-1, 0, 1})
            one_pass(NB - 1, 1, {-1, 0})
            one_pass(NB, 0, {-1})

        with nc.Block() as block:
            @block.tensor
            def _(pe):
                def one_pass(b, par, live):
                    for c in range(KF):
                        if 0 in live:
                            wait(pe, gelu_done, KF * b + c - 1)
                            for k in range(KD):
                                if c == 0:
                                    wait(pe, fn_lo, KD * b + k + 1)
                                for j, (a, d) in enumerate(PASSES):
                                    last = pe.matmul(HB[c % 2][:], r(w1_sb[:, a, k, c * P:(c + 1) * P]),
                                                     r(fnT[:, par, d, k, :]), start=(k == 0 and j == 0),
                                                     stop=(k == KD - 1 and j == 2))
                            last.then_inc(h_ready, 1)
                        rel, cc = (0, c - 1) if c else (-1, KF - 1)
                        if rel in live:
                            bb = b + rel
                            wait(pe, hid_lo, KF * bb + cc + 1)
                            for q in range(TT):
                                if cc == 0:
                                    wait(pe, acc_read, TT * bb)
                                for j, (a, d) in enumerate(PASSES):
                                    last = pe.matmul(ACC[q][:], r(hid[:, cc % 2, a, q * P:(q + 1) * P]),
                                                     r(w2_sb[:, d, cc, :]), start=(cc == 0 and j == 0),
                                                     stop=(cc == KF - 1 and j == 2))
                            last.then_inc(down_done, 1)
                        if c in TURN_AT and 1 in live:
                            f, bb = TURN_AT[c], b + 1
                            wait(pe, fz_done, TT * (bb + 1))
                            wait(pe, ft_copied, KD * bb + f - 1)
                            for q in range(TT):
                                last = pe.transpose(TB[f % 2][:, q * P:(q + 1) * P], yz[:, q, f * P:(f + 1) * P], ident[:])
                            last.then_inc(f_turned, 1)
                ffn_passes(pe, one_pass)

            @block.scalar
            def _(act):
                def one_pass(b, par, live):
                    for c in range(KF):
                        if 0 in live:
                            wait(act, h_ready, KF * b + c + 1)
                            wait(act, hid_lo, KF * b + c - 1)
                            act.activation(hid_full[:, c % 2, :], HB[c % 2][:], ACT.Gelu,
                                           bias=vec[:, col["b1"] + c:col["b1"] + c + 1]).then_inc(gelu_done, 1)
                        if c in TURN_AT and 1 in live:
                            f, bb = TURN_AT[c], b + 1
                            wait(act, f_turned, KD * bb + f + 1)
                            wait(act, fn_lo, KD * bb + f)
                            act.activation(ft[:], TB[f % 2][:], ACT.Identity, bias=mod[:, 1, 1, f, bass.ds(bb, 1)],
                                           scale=mod[:, 1, 0, f, bass.ds(bb, 1)]).then_inc(ft_copied, 1)
                ffn_passes(act, one_pass)

            @block.vector
            def _(dve):
                def one_pass(b, par, live):
                    for c in range(KF):
                        if 0 in live:
                            wait(dve, gelu_done, KF * b + c + 1)
                            wait(dve, down_done, KF * b + c - 1)
                            dve.tensor_copy(r(hid[:, c % 2, HI, :]), hid_full[:, c % 2, :]).then_inc(hid_hi, 1)
                            wait(dve, hid_hi, KF * b + c + 1)
                            dve.tensor_tensor(r(hid[:, c % 2, LO, :]), hid_full[:, c % 2, :], hid[:, c % 2, HI, :],
                                              ALU.subtract).then_inc(hid_lo, 1)
                        if c == 0 and -1 in live:
                            wait(dve, down_done, KF * b)
                            wait(dve, b2_added, TT * b)
                            for q in range(TT):
                                dve.tensor_tensor(res[:, 1 - par, q, :], ACC[q][:], res[:, 1 - par, q, :],
                                                  ALU.add).then_inc(acc_read, 1)
                        if c in (4, 5, 6, 7) and 1 in live:
                            i, bb = c - 4, b + 1
                            wait(dve, res_done, TT * bb + i + 1)
                            wait(dve, fmv_done, TT * bb)
                            dve.bn_stats(stats[:, i, :], res[:, 1 - par, i, :]).then_inc(fstats_done, 1)
                            waits(dve, half_done, (fstats_done, TT * bb + i + 1),
                                  (fz_done, TT * bb))
                            dve.bn_aggr(mean_var[:, i, :], stats[:, i, :]).then_inc(fmv_done, 1)
                        if c in TURN_AT and 1 in live:
                            f, bb = TURN_AT[c], b + 1
                            wait(dve, ft_copied, KD * bb + f + 1)
                            wait(dve, h_ready, KF * b)
                            dve.tensor_copy(r(fnT[:, 1 - par, HI, f, :]), ft[:]).then_inc(fn_hi, 1)
                            wait(dve, fn_hi, KD * bb + f + 1)
                            dve.tensor_tensor(r(fnT[:, 1 - par, LO, f, :]), ft[:], fnT[:, 1 - par, HI, f, :],
                                              ALU.subtract).then_inc(fn_lo, 1)
                ffn_passes(dve, one_pass)

            @block.gpsimd
            def _(pool):
                pool.wait_ge(bias_landed, 2 * DMA)

                def one_pass(b, par, live):
                    if 1 not in live:
                        return
                    bb, o = b + 1, 1 - par
                    wait(pool, in_landed[o], DMA * (bb + 2 - o))
                    for i in range(TT):
                        pool.tensor_tensor(res[:, o, i, :], res[:, o, i, :], yz[:, i, :], ALU.add).then_inc(summed, 1)
                    for i in range(TT):
                        wait(pool, summed, TT * bb + i + 1)
                        pool.tensor_tensor(res[:, o, i, :], res[:, o, i, :], bo_b[:], ALU.add).then_inc(res_done, 1)
                    waits(pool, half_done, (fmv_done, TT * (bb + 1)))
                    pool.tensor_scalar(neg_mean[:], mean_var[:, :, 0], -1.0, 0.0, ALU.mult, ALU.add).then_inc(fmoments_done, 1)
                    pool.tensor_scalar(var_eps[:], mean_var[:, :, 1], EPS, 1.0, ALU.add, ALU.mult).then_inc(fmoments_done, 1)
                    wait(pool, fmoments_done, 2 * (bb + 1))
                    pool.tensor_tensor(rstd[:], var_eps[:], minus_half[:], ALU.pow).then_inc(frstd_done, 1)
                    waits(pool, half_done, (frstd_done, bb + 1))
                    for i in range(TT):
                        pool.tensor_scalar(yz[:, i, :], res[:, o, i, :], neg_mean[:, i:i + 1], rstd[:, i:i + 1],
                                           ALU.add, ALU.mult).then_inc(fz_done, 1)
                    for i in range(TT):
                        pool.tensor_tensor(res[:, o, i, :], res[:, o, i, :], b2_b[:], ALU.add).then_inc(b2_added, 1)
                ffn_passes(pool, one_pass)

            @block.sync
            def _(sp):
                sp.dma_start(bo_b[:], bo.rearrange("(a d) -> a d", a=1).partition_broadcast(P)).then_inc(bias_landed, DMA)
                sp.dma_start(b2_b[:], b2.rearrange("(a d) -> a d", a=1).partition_broadcast(P)).then_inc(bias_landed, DMA)

                def one_pass(b, par, live):
                    if -1 in live:
                        bb = b - 1
                        for q in range(TT):
                            waits(sp, half_done, (acc_read, TT * bb + q + 1))
                            sp.dma_start(out_v[bass.ds(bb, 1), :, q, :].rearrange("o p d -> (o p) d"),
                                         res[:, 1 - par, q, :]).then_inc(out_stored[1 - par], DMA)
                    if 1 in live:
                        bb, o = b + 1, 1 - par
                        waits(sp, half_done, (out_stored[o], TT * DMA // 2 * (bb - o)),
                              (f_turned, KD * bb))
                        sp.dma_start(res[:, o], x_v[bass.ds(bb, 1)].rearrange("o p t d -> (o p) t d")).then_inc(in_landed[o], DMA)
                        sp.dma_start(yz[:], y_v[bass.ds(bb, 1)].rearrange("o p t d -> (o p) t d")).then_inc(in_landed[o], DMA)
                ffn_passes(sp, one_pass)
                for i in range(2):
                    sp.wait_ge(out_stored[i], TT * DMA * NB // 2)
        part2.close()


_INS = ["x", "cond_1024"] + ["L0_cond_" + n for n in (
    "ln1_w", "ln1_b", "ln2_w", "ln2_b", "wq", "bq", "wk", "bk", "wv", "bv", "wo", "bo",
    "wt_attn", "bt_attn", "wt_ffn", "bt_ffn", "w1", "b1", "w2", "b2")]


def kernel(**inputs):
    import numpy as _np
    import concourse.bacc as _bacc
    from concourse import mybir as _mybir
    from concourse.bass_utils import run_bass_kernel_spmd as _run

    nc = _bacc.Bacc("TRN2", target_bir_lowering=False, num_devices=1)
    arrays, args = {}, []
    for name in _INS:
        a = _np.ascontiguousarray(inputs[name])
        arrays[f"in_{name}_dram"] = a
        args.append(nc.dram_tensor(f"in_{name}_dram", a.shape, _mybir.dt.from_np(a.dtype), kind="ExternalInput").ap())
    shape = arrays["in_x_dram"].shape
    args.append(nc.dram_tensor("attn_out_dram", shape, _mybir.dt.float32, kind="Internal").ap())
    args.append(nc.dram_tensor("out_0_dram", shape, _mybir.dt.float32, kind="ExternalOutput").ap())
    conditioned_layer(nc, *args)
    res = _run(nc, [arrays], core_ids=[0])
    return res.results[0]["out_0_dram"]
```

```python
from contextlib import ExitStack

import concourse.bass as bass
from concourse import mybir

ALU = mybir.AluOpType
ACT = mybir.ActivationFunctionType
AX = mybir.AxisListType
F32 = mybir.dt.float32
F32R = mybir.dt.float32r

P = 128
HI, LO = 0, 1
PASSES = [(HI, HI), (HI, LO), (LO, HI)]
Q_LO, Q_HI, K_HI, K_LO = range(4)
STACK_PARTS = [slice(Q_HI, K_HI + 1), slice(Q_LO, K_HI + 1, 2), slice(Q_HI, K_LO + 1, 2)]
EPS = 1e-5
DMA = 16


def r(ap):
    return ap.bitcast(F32R)


def wait(eng, sem, value):
    if isinstance(value, int) and value <= 0:
        return
    eng.wait_ge(sem, value)


def is_batch(b, n):
    return isinstance(b, int) and b == n


def waits(eng, met, *pairs):
    for _, value in pairs:
        if not isinstance(value, int):
            eng.compute_val(value)
    eng.wait_ge(met, 1)
    for sem, value in pairs:
        wait(eng, sem, value)


def conditioned_layer(nc, x, cond, ln1_w, ln1_b, ln2_w, ln2_b, wq, bq, wk, bk, wv, bv, wo, bo,
                      wt_attn, bt_attn, wt_ffn, bt_ffn, w1, b1, w2, b2, attn_out, out):
    NB, T, D = x.shape
    F = w1.shape[1]
    HD = 32
    NH = D // HD
    TT = T // P
    KD = D // P
    KF = F // P
    HG = P // HD
    NG = NH // HG
    RING = 8
    SUB = 4
    VW = 2 * HD + 1
    SCALE = float(HD) ** -0.5
    assert TT == SUB and KD == SUB and NG == SUB and NH == 16 and T == 512 and D == 512

    VECS = [("ln1_w", ln1_w), ("ln1_b", ln1_b), ("ln2_w", ln2_w), ("ln2_b", ln2_b), ("bq", bq), ("bk", bk),
            ("bv", bv), ("bt_attn", bt_attn), ("bt_ffn", bt_ffn), ("b1", b1)]
    col, n_vec = {}, 0
    for name, v in VECS:
        col[name] = n_vec
        n_vec += v.shape[0] // P

    x_v = x.rearrange("b (t p) d -> b p t d", p=P)
    y_v = attn_out.rearrange("b (t p) d -> b p t d", p=P)
    out_v = out.rearrange("b (t p) d -> b p t d", p=P)

    with ExitStack() as whole:
        def sb(ctx, name, shape):
            return ctx.enter_context(nc.sbuf_tensor(name, shape, F32))

        def sem(name):
            return whole.enter_context(nc.semaphore(name))

        ident = sb(whole, "ident", [P, P])
        vec = sb(whole, "vec", [P, n_vec])
        mod = sb(whole, "mod", [P, 2, 2, KD, NB])
        minus_half = sb(whole, "minus_half", [P, TT])
        stats = sb(whole, "stats", [P, TT, 6])
        mean_var = sb(whole, "mean_var", [P, TT, 2])
        neg_mean = sb(whole, "neg_mean", [P, TT])
        var_eps = sb(whole, "var_eps", [P, TT])
        rstd = sb(whole, "rstd", [P, TT])
        xz = sb(whole, "xz", [P, TT, D])
        xt = sb(whole, "xt", [P, T])
        xnT = sb(whole, "xnT", [P, 2, KD, T])
        staging = sb(whole, "staging", [P, 4, T])
        res = [staging]
        bo_b = sb(whole, "bo_b", [P, D])
        ps = [whole.enter_context(nc.psum_tensor(f"ps{i}", [P, 512], F32)) for i in range(8)]

        part1 = ExitStack()
        w_at = {n: sb(part1, f"w_{n}", [P, 2, KD, D]) for n in ("q", "k", "v", "o")}

        scratch = ExitStack()
        vec_rows = sb(scratch, "vec_rows", [n_vec, P])
        cond_rows = sb(scratch, "cond_rows", [NB, D])
        condT = sb(scratch, "condT", [P, KD, NB])
        one_plus = sb(scratch, "one_plus", [P, NB])
        shift_part = sb(scratch, "shift_part", [P, NB])
        t_rows = sb(scratch, "t_rows", [NB, 2, 2 * D])
        wt_raw = [sb(scratch, f"wt_raw{i}", [P, KD, 2 * D]) for i in range(2)]
        w_raw = {n: sb(scratch, f"w_raw_{n}", [P, KD, D]) for n in w_at}

        vec_landed, cond_landed = sem("vec_landed"), sem("cond_landed")
        wt_landed = [sem(f"wt_landed{i}") for i in range(2)]
        w_landed = {n: sem(f"w_landed_{n}") for n in w_at}
        ident_zero, ident_done, half_done = sem("ident_zero"), sem("ident_done"), sem("half_done")
        vec_turned, vec_done, cond_turned, condT_done = sem("vec_turned"), sem("vec_done"), sem("cond_turned"), sem("condT_done")
        t_ready, t_copied, mod_ready, mod_step = sem("t_ready"), sem("t_copied"), sem("mod_ready"), sem("mod_step")
        w_hi_done, w_lo_done = sem("w_hi_done"), sem("w_lo_done")
        x_landed, stats_done, mv_done = sem("x_landed"), sem("stats_done"), sem("mv_done")
        moments_done, rstd_done, z_done = sem("moments_done"), sem("rstd_done"), sem("z_done")
        in_landed = [sem(f"in_landed{i}") for i in range(2)]
        bias_landed, summed, res_done = sem("bias_landed"), sem("summed"), sem("res_done")
        fstats_done, fmv_done, fmoments_done = sem("fstats_done"), sem("fmv_done"), sem("fmoments_done")
        frstd_done, fz_done, f_turned = sem("frstd_done"), sem("fz_done"), sem("f_turned")
        ft_copied, fn_hi, fn_lo = sem("ft_copied"), sem("fn_hi"), sem("fn_lo")

        def moments_and_rows(pool, bb, sems, rows_in, rows_out):
            mv, moments, rs, z = sems
            waits(pool, half_done, (mv, TT * (bb + 1)))
            pool.tensor_scalar(neg_mean[:], mean_var[:, :, 0], -1.0, 0.0, ALU.mult, ALU.add).then_inc(moments, 1)
            pool.tensor_scalar(var_eps[:], mean_var[:, :, 1], EPS, 1.0, ALU.add, ALU.mult).then_inc(moments, 1)
            wait(pool, moments, 2 * (bb + 1))
            pool.tensor_tensor(rstd[:], var_eps[:], minus_half[:], ALU.pow).then_inc(rs, 1)
            waits(pool, half_done, (rs, bb + 1))
            for i in range(TT):
                pool.tensor_scalar(rows_out[:, i, :], rows_in[:, i, :], neg_mean[:, i:i + 1], rstd[:, i:i + 1],
                                   ALU.add, ALU.mult).then_inc(z, 1)
        ATTN_NORM, FFN_NORM = (mv_done, moments_done, rstd_done, z_done), (fmv_done, fmoments_done, frstd_done, fz_done)

        with nc.Block() as block:
            @block.sync
            def _(sp):
                sp.dma_start(cond_rows[:], cond).then_inc(cond_landed, DMA)
                for i, w in enumerate((wt_attn, wt_ffn)):
                    sp.dma_start(wt_raw[i][:], w.rearrange("(k p) n -> p k n", p=P)).then_inc(wt_landed[i], DMA)
                    if i == 0:
                        for name, v in VECS:
                            n = v.shape[0] // P
                            sp.dma_start(vec_rows[col[name]:col[name] + n, :],
                                         v.rearrange("(r c) -> r c", c=P)).then_inc(vec_landed, DMA)
                sp.dma_start(xz[:], x_v[0:1].rearrange("o p t d -> (o p) t d")).then_inc(x_landed, DMA)
                for n, w in (("k", wk), ("q", wq), ("v", wv), ("o", wo)):
                    sp.dma_start(w_raw[n][:], w.rearrange("(k p) n -> p k n", p=P)).then_inc(w_landed[n], DMA)
                sp.wait_ge(w_lo_done, 4)

            @block.gpsimd
            def _(pool):
                pool.memset(ident[:], 0.0).then_inc(ident_zero, 1)
                pool.wait_ge(ident_zero, 1)
                pool.affine_select(out=ident[:], in_=ident[:], compare_op=ALU.not_equal, fill=1.0, base=0,
                                   pattern=[[-1, P]], channel_multiplier=1).then_inc(ident_done, 1)
                pool.memset(minus_half[:], -0.5).then_inc(half_done, 1)
                moments_and_rows(pool, 0, ATTN_NORM, xz, xz)

            @block.tensor
            def _(pe):
                pe.wait_ge(ident_done, 1)
                pe.wait_ge(cond_landed, DMA)
                for k in range(KD):
                    last = pe.transpose(ps[1][:, k * NB:(k + 1) * NB], cond_rows[:, k * P:(k + 1) * P],
                                        ident[0:NB, 0:NB])
                last.then_inc(cond_turned, 1)
                pe.wait_ge(condT_done, 1)
                for i in range(2):
                    pe.wait_ge(wt_landed[i], DMA)
                    for h in range(2):
                        for k in range(KD):
                            last = pe.matmul(ps[2 + 2 * i + h][0:NB, :], condT[:, k, :], wt_raw[i][:, k, h * D:(h + 1) * D],
                                             start=(k == 0), stop=(k == KD - 1))
                        last.then_inc(t_ready, 1)
                    if i == 0:
                        pe.wait_ge(vec_landed, DMA * len(VECS))
                        pe.transpose(ps[0][:, 0:n_vec], vec_rows[:], ident[0:n_vec, 0:n_vec]).then_inc(vec_turned, 1)
                    pe.wait_ge(t_copied, 2 * (i + 1))
                    for m in range(2 * KD):
                        last = pe.transpose(ps[6 + i][:, m * NB:(m + 1) * NB], t_rows[:, i, m * P:(m + 1) * P],
                                            ident[0:NB, 0:NB])
                    last.then_inc(mod_ready, 1)

            @block.scalar
            def _(act):
                for n in ("k", "q", "v", "o"):
                    act.wait_ge(w_landed[n], DMA)
                    act.activation(r(w_at[n][:, HI]), w_raw[n][:], ACT.Copy).then_inc(w_hi_done, 1)

            @block.vector
            def _(dve):
                def split(i):
                    n = ("k", "q", "v", "o")[i]
                    dve.wait_ge(w_hi_done, i + 1)
                    dve.tensor_tensor(r(w_at[n][:, LO]), w_raw[n][:], w_at[n][:, HI], ALU.subtract).then_inc(w_lo_done, 1)

                def copy_t(i):
                    for h in range(2):
                        dve.wait_ge(t_ready, 2 * i + h + 1)
                        dve.tensor_copy(t_rows[:, i, h * D:(h + 1) * D], ps[2 + 2 * i + h][0:NB, :]).then_inc(t_copied, 1)

                def modulation(i):
                    w_c, b_c, t_c = [[col[n] for n in names] for names in (("ln1_w", "ln1_b", "bt_attn"),
                                                                          ("ln2_w", "ln2_b", "bt_ffn"))][i]
                    dve.wait_ge(mod_ready, i + 1)
                    for f in range(KD):
                        step = 4 * (KD * i + f)
                        shift_ps = ps[6 + i][:, f * NB:(f + 1) * NB]
                        scale_ps = ps[6 + i][:, (KD + f) * NB:(KD + f + 1) * NB]
                        dve.tensor_scalar(one_plus[:], scale_ps, vec[:, t_c + KD + f:t_c + KD + f + 1], 1.0,
                                          ALU.add, ALU.add).then_inc(mod_step, 1)
                        dve.wait_ge(mod_step, step + 1)
                        dve.tensor_scalar(mod[:, i, 0, f, :], one_plus[:], vec[:, w_c + f:w_c + f + 1], None,
                                          ALU.mult).then_inc(mod_step, 1)
                        dve.tensor_scalar(shift_part[:], one_plus[:], vec[:, b_c + f:b_c + f + 1],
                                          vec[:, t_c + f:t_c + f + 1], ALU.mult, ALU.add).then_inc(mod_step, 1)
                        dve.wait_ge(mod_step, step + 3)
                        dve.tensor_tensor(mod[:, i, 1, f, :], shift_part[:], shift_ps, ALU.add).then_inc(mod_step, 1)
                        dve.wait_ge(mod_step, step + 4)

                dve.wait_ge(cond_turned, 1)
                dve.tensor_copy(condT[:].rearrange("p k b -> p (k b)"), ps[1][:, 0:KD * NB]).then_inc(condT_done, 1)
                copy_t(0)
                dve.wait_ge(vec_turned, 1)
                dve.tensor_copy(vec[:], ps[0][:, 0:n_vec]).then_inc(vec_done, 1)
                dve.wait_ge(vec_done, 1)
                dve.wait_ge(x_landed, DMA)
                for i in range(TT):
                    dve.bn_stats(stats[:, i, :], xz[:, i, :]).then_inc(stats_done, 1)
                for i in range(TT):
                    dve.wait_ge(stats_done, i + 1)
                    dve.bn_aggr(mean_var[:, i, :], stats[:, i, :]).then_inc(mv_done, 1)
                copy_t(1)
                modulation(0)
                split(0)
                split(1)
                modulation(1)
                split(2)
                split(3)

        scratch.close()

        stack = sb(part1, "stack", [P, RING, 2, T])
        v_op = sb(part1, "v_op", [P, TT, NH, VW])
        p_full = sb(part1, "p_full", [P, 2, T])
        p_hi = sb(part1, "p_hi", [P, 4, T])
        p_lo = sb(part1, "p_lo", [P, 4, T])
        u_sb = sb(part1, "u_sb", [VW, 2, T])
        halves = sb(part1, "halves", [P, 2, 2, T])
        recip_b = sb(part1, "recip_b", [P, T])
        rows = sb(part1, "rows", [P, T])
        sums = sb(part1, "sums", [HG * 16, T // 16])
        recips = sb(part1, "recips", [HG * 16, T // 16])
        attnT = sb(part1, "attnT", [P, 2, NG, T])
        y_sb = sb(part1, "y_sb", [P, 2, D])
        neg_max = sb(part1, "neg_max", [P, 2, TT, 2])

        ST, S, G, TR, U = ps[0:2], ps[2:4], ps[4:6], ps[6], ps[7]

        def whole_slot(t):
            return [SUB * t + s for s in range(SUB)]
        UNITS = [("k", 0, 2, whole_slot(0)), ("q", 0, 2, whole_slot(1)), ("v", 0, 2, whole_slot(2)),
                 ("v", 0, 3, whole_slot(3)), ("k", 0, 3, whole_slot(4)), ("q", 0, 3, whole_slot(5)),
                 ("o", -1, 0, [24, 25, 26]), ("o", -1, 1, [27, 28, 29]), ("o", -1, 2, [30, 31, 32]),
                 ("o", -1, 3, [33, 34, 35]), ("k", 1, 0, whole_slot(9)), ("q", 1, 0, whole_slot(10)),
                 ("v", 1, 0, whole_slot(11)), ("k", 1, 1, whole_slot(12)), ("q", 1, 1, whole_slot(13)),
                 ("v", 1, 1, [56, 58, 60, 61])]
        EVACUATED_AT = {i: subs[-1] + 1 for i, (_, _, _, subs) in enumerate(UNITS)}
        EVACUATED_AT[13] = 53
        TURNS = sorted([(SUB * t + 1, "neg", (t + 2) // NH, (t + 2) % NH // 2) for t in range(0, NH, 2)]
                       + [(27, "x", 1, 0), (29, "x", 1, 1), (31, "x", 1, 2), (35, "x", 1, 3)])
        X_COPY_AT = {28: 0, 30: 1, 32: 2, 36: 3}
        ATTN_AT = {37: (0, 0), 49: (0, 1), 1: (-1, 2), 17: (-1, 3)}
        RECIP_AT = {23: (0, 0), 39: (0, 1), 55: (0, 2), 7: (-1, 3)}
        STACK_AT = {0: [(0, 7)], 10: [(0, 8)], 11: [(0, 9)], 13: [(0, 10)], 16: [(0, 11)],
                    26: [(0, 12)], 27: [(0, 13)], 29: [(0, 14)], 32: [(0, 15)],
                    45: [(1, 0)], 47: [(1, 1)], 48: [(1, 2)], 49: [(1, 3)],
                    57: [(1, 4)], 58: [(1, 5)], 60: [(1, 6)]}

        st_ready, exp_done, split_done, av_done = sem("st_ready"), sem("exp_done"), sem("split_done"), sem("av_done")
        s_ready, max_done = sem("s_ready"), sem("max_done")
        neg_turned, neg_copied = sem("neg_turned"), sem("neg_copied")
        neg_landed = [sem(f"neg_landed{i}") for i in range(2)]
        u_copied, halves_added, normed = sem("u_copied"), sem("halves_added"), sem("normed")
        halves_landed = [sem(f"halves_landed{i}") for i in range(2)]
        sum_landed = [sem(f"sum_landed{i}") for i in range(2)]
        recip_done, recip_row_landed, recip_b_landed = sem("recip_done"), sem("recip_row_landed"), sem("recip_b_landed")
        attn_hi, attn_lo = sem("attn_hi"), sem("attn_lo")
        x_turned, xt_copied, xn_hi, xn_lo = sem("x_turned"), sem("xt_copied"), sem("xn_hi"), sem("xn_lo")
        qk_ready, qk_hi, qk_lo = sem("qk_ready"), sem("qk_hi"), sem("qk_lo")
        stack_landed = [sem(f"stack_landed{i}") for i in range(RING)]
        v_ready, v_hi, v_lo = sem("v_ready"), sem("v_hi"), sem("v_lo")
        o_ready, y_copied = sem("o_ready"), sem("y_copied")
        y_stored = [sem(f"y_stored{i}") for i in range(2)]

        def unit_index(kind, b, n):
            if kind in "qk":
                return 2 * KD * b + 2 * n + (kind == "q")
            return 4 * b + n

        def unit_exists(live, i):
            return UNITS[i][1] in live

        def bank_freed(b, live, i):
            freed = {"k": qk_lo, "q": qk_lo, "v": v_lo, "o": y_copied}
            j, back = i - 2, 0
            while True:
                if j < 0:
                    j, back = j + len(UNITS), back + 1
                kind, rel, n, _ = UNITS[j]
                if isinstance(b, int):
                    if b - back < -1:
                        return freed[kind], 0
                    if not 0 <= b - back + rel < NB:
                        j -= 2
                        continue
                return freed[kind], unit_index(kind, b - back + rel, n) + 1

        def turn_bank_freed(b, i):
            freed = {"neg": neg_copied, "x": xt_copied}
            j, back = i - 1, 0
            while True:
                if j < 0:
                    j, back = j + len(TURNS), back + 1
                _, kind, rel, n = TURNS[j]
                if isinstance(b, int):
                    if b - back < -1:
                        return freed[kind], 0
                    if not 0 <= b - back + rel < NB:
                        j -= 1
                        continue
                return freed[kind], (8 if kind == "neg" else KD) * (b - back + rel) + n + 1

        def passes(eng, one_pass):
            one_pass(-1, {1})
            one_pass(0, {0, 1})
            one_pass(1, {-1, 0, 1})
            with eng.Fori(2, NB - 1) as b:
                one_pass(b, {-1, 0, 1})
            one_pass(NB - 1, {-1, 0})
            one_pass(NB, {-1})

        def lagging(tau, lag):
            u = tau - lag
            return (0 if u >= 0 else -1), (u % 64) // SUB, u % SUB

        ones_done = sem("ones_done")
        FIRST_IN_AT = 36
        FIRST_SUM_AT, FIRST_BIAS_AT = {44: 0, 45: 1, 46: 2, 47: 3}, {48: 0, 49: 1, 50: 2, 51: 3}
        FIRST_STATS_AT = {52: 0, 53: 1, 54: 2, 55: 3}
        FIRST_TURN_AT = {3: 0, 5: 1, 7: 2, 9: 3}

        with nc.Block() as block:
            @block.tensor
            def _(pe):
                pe.wait_ge(ones_done, 2)

                def project(b, i, part):
                    kind, rel, n, subs = UNITS[i]
                    bank, bb = G[i % 2], b + rel
                    if part == 0:
                        wait(pe, *bank_freed(b, None, i))
                    if kind in "qk":
                        if kind == "k" and n == 0:
                            wait(pe, xn_lo, KD * bb + part + 1)
                        for j, (a, c) in enumerate(PASSES):
                            last = pe.matmul(bank[:], r(w_at[kind][:, a, part, n * P:(n + 1) * P]),
                                             r(xnT[:, c, part, :]), start=(part == 0 and j == 0),
                                             stop=(part == KD - 1 and j == 2))
                        if part == KD - 1:
                            last.then_inc(qk_ready, 1)
                    elif kind == "v":
                        half, tile = n // 2, 2 * (n % 2) + part // 2
                        o = bank[:, (part // 2) * 256:(part // 2) * 256 + 256]
                        for k in (2 * (part % 2), 2 * (part % 2) + 1):
                            for j, (a, c) in enumerate(PASSES):
                                last = pe.matmul(o, r(xnT[:, a, k, tile * P:(tile + 1) * P]),
                                                 r(w_at["v"][:, c, k, half * 256:half * 256 + 256]),
                                                 start=(k == 0 and j == 0), stop=(k == KD - 1 and j == 2))
                        if part == 3:
                            last.then_inc(v_ready, 1)
                    else:
                        for m in range(4 * part, 4 * part + 4):
                            g, j = m // 3, m % 3
                            a, c = PASSES[j]
                            if n == 0 and j == 0:
                                wait(pe, attn_lo, NG * bb + g + 1)
                            last = pe.matmul(bank[:], r(attnT[:, a, g, n * P:(n + 1) * P]),
                                             r(w_at["o"][:, c, g, :]), start=(m == 0), stop=(m == 11))
                        if part == 2:
                            last.then_inc(o_ready, 1)

                def attend(b, live, tau):
                    rel, h, kt = lagging(tau, 3)
                    if rel in live:
                        n = 64 * (b + rel) + SUB * h + kt
                        wait(pe, split_done, n + 1)
                        if kt == 0:
                            wait(pe, u_copied, NH * (b + rel) + h)
                        if kt == 0 and h % 8 == 0:
                            wait(pe, v_lo, 4 * (b + rel) + 2 + h // 4)
                        pe.matmul(U[0:VW, :], r(v_op[:, kt, h, :]), r(p_hi[:, kt, :]),
                                  start=(kt == 0), stop=False)
                        pe.matmul(U[0:VW, :], r(v_op[:, kt, h, :]), r(p_lo[:, kt, :]),
                                  start=False, stop=(kt == TT - 1)).then_inc(av_done, 1)

                def one_pass(b, live):
                    for tau in range(64):
                        t, s = tau // SUB, tau % SUB
                        if 0 in live:
                            n = 64 * b + tau
                            wait(pe, exp_done, n - 1)
                            if s == 0 and t % 2 == 0:
                                wait(pe, neg_landed[t // 2 % 2], DMA * (4 * b + t // 4 + 1))
                            pe.matmul(ST[tau % 2][:], r(stack[0:97, t % RING, 1, s * P:(s + 1) * P]),
                                      r(stack[0:97, t % RING, 0, :]), start=True, stop=True).then_inc(st_ready, 1)
                        rel, h = (t + 4) // NH, (t + 4) % NH
                        if rel in live:
                            m = 64 * (b + rel) + SUB * h + s
                            wait(pe, max_done, m - 1)
                            if s == 0:
                                wait(pe, stack_landed[h % RING], 3 * DMA * (2 * (b + rel) + h // RING + 1))
                            pe.matmul(S[tau % 2][:], r(stack[0:96, h % RING, 0, s * P:(s + 1) * P]),
                                      r(stack[0:96, h % RING, 1, :]), start=True, stop=True).then_inc(s_ready, 1)
                        if s == 2:
                            attend(b, live, tau)
                        for i, (_, rel, _, subs) in enumerate(UNITS):
                            if tau in subs and rel in live:
                                project(b, i, subs.index(tau))
                        for i, (at, kind, rel, n) in enumerate(TURNS):
                            if at != tau or rel not in live:
                                continue
                            if kind == "neg":
                                wait(pe, max_done, 64 * (b + rel) + 8 * n + 8)
                                wait(pe, *turn_bank_freed(b, i))
                                for q in range(TT):
                                    last = pe.transpose(TR[0:2, q * P:(q + 1) * P], neg_max[:, n % 2, q, :], ident[:])
                                last.then_inc(neg_turned, 1)
                            else:
                                wait(pe, z_done, TT * (b + rel + 1))
                                wait(pe, *turn_bank_freed(b, i))
                                for q in range(TT):
                                    last = pe.transpose(TR[:, q * P:(q + 1) * P], xz[:, q, n * P:(n + 1) * P], ident[:])
                                last.then_inc(x_turned, 1)
                        if s != 2:
                            attend(b, live, tau)
                        if is_batch(b, NB) and tau in FIRST_TURN_AT:
                            f = FIRST_TURN_AT[tau]
                            wait(pe, fz_done, TT)
                            wait(pe, neg_copied, 8 * NB)
                            wait(pe, ft_copied, f)
                            for q in range(TT):
                                last = pe.transpose(TR[:, q * P:(q + 1) * P], xz[:, q, f * P:(f + 1) * P], ident[:])
                            last.then_inc(f_turned, 1)

                passes(pe, one_pass)

            @block.scalar
            def _(act):
                def evacuate(b, i):
                    kind, rel, n, _ = UNITS[i]
                    bank, bb = G[i % 2], b + rel
                    if kind in "qk":
                        wait(act, qk_ready, unit_index(kind, bb, n) + 1)
                        if kind == "k":
                            for j in range(HG):
                                wait(act, stack_landed[(n + 1) % 2 * HG + j], 3 * DMA * (2 * bb + (n + 1) // 2))
                        part, bias = (K_HI, col["bk"]) if kind == "k" else (Q_HI, col["bq"])
                        act.activation(r(staging[:, part, :]), bank[:], ACT.Identity,
                                       bias=vec[:, bias + n:bias + n + 1]).then_inc(qk_hi, 1)
                    elif kind == "v":
                        wait(act, v_ready, 4 * bb + n + 1)
                        wait(act, av_done, 64 * bb - 32 if n < 2 else 64 * bb)
                        k, h = 2 * (n % 2), 8 * (n // 2)
                        act.activation(r(v_op[:, k:k + 2, h:h + 8, 0:HD]),
                                       bank[:].rearrange("p (k h e) -> p k h e", k=2, h=8), ACT.Copy).then_inc(v_hi, 1)
                    else:
                        wait(act, o_ready, 4 * bb + n + 1)
                        wait(act, y_stored[n % 2], DMA * (2 * bb + n // 2))
                        act.activation(y_sb[:, n % 2, :], bank[:], ACT.Copy).then_inc(y_copied, 1)

                def one_pass(b, live):
                    for tau in range(64):
                        t, s = tau // SUB, tau % SUB
                        if 0 in live:
                            n = 64 * b + tau
                            wait(act, st_ready, n + 1)
                            wait(act, av_done, n - 3)
                            act.activation(r(p_hi[:, tau % 4, :]), ST[tau % 2][:], ACT.Exp, scale=SCALE)
                        if s == 2:
                            rel, h = (0, t - 1) if t >= 1 else (-1, NH - 1)
                            if rel in live:
                                bb = b + rel
                                wait(act, av_done, 64 * bb + SUB * h + 4)
                                wait(act, halves_landed[h % 2], 2 * DMA * (8 * bb + h // 2))
                                wait(act, sum_landed[h % 2], DMA * (8 * bb + h // 2))
                                act.activation(u_sb[:, h % 2, :], U[0:VW, :], ACT.Copy).then_inc(u_copied, 1)
                        if 0 in live:
                            wait(act, split_done, n - 1)
                            act.activation(p_full[:, tau % 2, :], ST[tau % 2][:], ACT.Exp,
                                           scale=SCALE).then_inc(exp_done, 1)
                        for at, kind, rel, n in TURNS:
                            if kind == "neg" and at + 1 == tau and rel in live:
                                bb = b + rel
                                wait(act, neg_turned, 8 * bb + n + 1)
                                wait(act, neg_landed[n % 2], DMA * (4 * bb + n // 2))
                                p0 = 64 * (n % 2)
                                act.activation(r(rows[p0:p0 + 2, :]), TR[0:2, :], ACT.Copy).then_inc(neg_copied, 1)
                        if tau in X_COPY_AT and 1 in live:
                            f, bb = X_COPY_AT[tau], b + 1
                            wait(act, x_turned, KD * bb + f + 1)
                            wait(act, xn_lo, KD * bb + f)
                            act.activation(xt[:], TR[:], ACT.Identity, bias=mod[:, 0, 1, f, bass.ds(bb, 1)],
                                           scale=mod[:, 0, 0, f, bass.ds(bb, 1)]).then_inc(xt_copied, 1)
                        if is_batch(b, NB) and tau - 1 in FIRST_TURN_AT:
                            f = FIRST_TURN_AT[tau - 1]
                            wait(act, f_turned, f + 1)
                            wait(act, xn_lo, KD * NB)
                            wait(act, fn_lo, f)
                            act.activation(xt[:], TR[:], ACT.Identity, bias=mod[:, 1, 1, f, 0:1],
                                           scale=mod[:, 1, 0, f, 0:1]).then_inc(ft_copied, 1)
                        for i, (_, rel, _, _) in enumerate(UNITS):
                            if EVACUATED_AT[i] == tau and rel in live:
                                evacuate(b, i)
                        if tau in ATTN_AT and ATTN_AT[tau][0] in live:
                            rel, g = ATTN_AT[tau]
                            bb = b + rel
                            wait(act, normed, NG * bb + g + 1)
                            wait(act, o_ready, 4 * bb)
                            act.activation(r(attnT[:, HI, g, :]), halves[:, g % 2, 0, :], ACT.Identity,
                                           bias=vec[:, col["bv"] + g:col["bv"] + g + 1]).then_inc(attn_hi, 1)

                passes(act, one_pass)

            @block.vector
            def _(dve):
                dve.memset(v_op[:, :, :, 2 * HD:VW], 1.0).then_inc(ones_done, 1)
                dve.memset(stack[96:97, :, 1, :], 1.0).then_inc(ones_done, 1)

                def evacuate(b, i):
                    kind, rel, n, _ = UNITS[i]
                    bank, bb = G[i % 2], b + rel
                    if kind in "qk":
                        wait(dve, qk_hi, unit_index(kind, bb, n) + 1)
                        hi, lo, bias = (K_HI, K_LO, col["bk"]) if kind == "k" else (Q_HI, Q_LO, col["bq"])
                        dve.scalar_tensor_tensor(r(staging[:, lo, :]), bank[:], vec[:, bias + n:bias + n + 1],
                                                 staging[:, hi, :], ALU.add, ALU.subtract).then_inc(qk_lo, 1)
                    elif kind == "v":
                        wait(dve, v_hi, 4 * bb + n + 1)
                        k, h = 2 * (n % 2), 8 * (n // 2)
                        dve.tensor_tensor(r(v_op[:, k:k + 2, h:h + 8, HD:2 * HD]),
                                          bank[:].rearrange("p (k h e) -> p k h e", k=2, h=8),
                                          v_op[:, k:k + 2, h:h + 8, 0:HD], ALU.subtract).then_inc(v_lo, 1)

                def first_batch_rows(tau):
                    if tau in FIRST_SUM_AT:
                        i = FIRST_SUM_AT[tau]
                        wait(dve, in_landed[0], 2 * DMA)
                        dve.tensor_tensor(staging[:, i, :], staging[:, i, :], xz[:, i, :], ALU.add).then_inc(summed, 1)
                    if tau in FIRST_BIAS_AT:
                        i = FIRST_BIAS_AT[tau]
                        wait(dve, summed, i + 1)
                        wait(dve, bias_landed, DMA)
                        dve.tensor_tensor(staging[:, i, :], staging[:, i, :], bo_b[:], ALU.add).then_inc(res_done, 1)
                    if tau in FIRST_STATS_AT:
                        i = FIRST_STATS_AT[tau]
                        wait(dve, res_done, i + 1)
                        if i == 0:
                            wait(dve, z_done, TT * NB)
                        dve.bn_stats(stats[:, i, :], staging[:, i, :]).then_inc(fstats_done, 1)
                        dve.wait_ge(fstats_done, i + 1)
                        dve.bn_aggr(mean_var[:, i, :], stats[:, i, :]).then_inc(fmv_done, 1)

                def one_pass(b, live):
                    for tau in range(64):
                        t, s = tau // SUB, tau % SUB
                        for i, (_, rel, _, _) in enumerate(UNITS):
                            if EVACUATED_AT[i] + 1 == tau and rel in live:
                                evacuate(b, i)
                        rel, h = (t + 4) // NH, (t + 4) % NH
                        if rel in live:
                            bb = b + rel
                            wait(dve, s_ready, 64 * bb + SUB * h + s + 1)
                            if s == 0 and h % 2 == 0:
                                wait(dve, neg_turned, 8 * bb + h // 2 - 1)
                            dve.tensor_reduce(neg_max[:, h // 2 % 2, s, h % 2:h % 2 + 1], S[tau % 2][:], AX.X,
                                              ALU.max, negate=True).then_inc(max_done, 1)
                        rel, h, kt = lagging(tau, 1)
                        if rel in live:
                            n = 64 * (b + rel) + SUB * h + kt
                            wait(dve, exp_done, n + 1)
                            dve.tensor_tensor(r(p_lo[:, kt, :]), p_full[:, kt % 2, :], p_hi[:, kt, :],
                                              ALU.subtract).then_inc(split_done, 1)
                        if 1 in live and not is_batch(b, -1) and tau in (8, 10, 12, 14):
                            i = (tau - 8) // 2
                            wait(dve, x_landed, DMA * (b + 2))
                            wait(dve, mv_done, TT * (b + 1))
                            dve.bn_stats(stats[:, i, :], xz[:, i, :]).then_inc(stats_done, 1)
                        if 1 in live and not is_batch(b, -1) and tau in (9, 11, 13, 15):
                            i = (tau - 9) // 2
                            waits(dve, half_done, (stats_done, TT * (b + 1) + i + 1),
                                  (z_done, TT * (b + 1)))
                            dve.bn_aggr(mean_var[:, i, :], stats[:, i, :]).then_inc(mv_done, 1)
                        if tau - 1 in X_COPY_AT and 1 in live:
                            f, bb = X_COPY_AT[tau - 1], b + 1
                            if f == 0:
                                wait(dve, qk_ready, 2 * KD * bb)
                                wait(dve, v_ready, 4 * bb)
                            wait(dve, xt_copied, KD * bb + f + 1)
                            dve.tensor_copy(r(xnT[:, HI, f, :]), xt[:]).then_inc(xn_hi, 1)
                            wait(dve, xn_hi, KD * bb + f + 1)
                            dve.tensor_tensor(r(xnT[:, LO, f, :]), xt[:], xnT[:, HI, f, :],
                                              ALU.subtract).then_inc(xn_lo, 1)
                        if is_batch(b, NB - 1):
                            first_batch_rows(tau)
                        if is_batch(b, NB) and tau - 2 in FIRST_TURN_AT:
                            f = FIRST_TURN_AT[tau - 2]
                            wait(dve, qk_ready, 2 * KD * NB)
                            wait(dve, v_ready, 4 * NB)
                            wait(dve, ft_copied, f + 1)
                            dve.tensor_copy(r(xnT[:, HI, f, :]), xt[:]).then_inc(fn_hi, 1)
                            wait(dve, fn_hi, f + 1)
                            dve.tensor_tensor(r(xnT[:, LO, f, :]), xt[:], xnT[:, HI, f, :],
                                              ALU.subtract).then_inc(fn_lo, 1)
                        if tau in RECIP_AT and RECIP_AT[tau][0] in live:
                            rel, g = RECIP_AT[tau]
                            bb = b + rel
                            for i in range(2):
                                wait(dve, sum_landed[i], DMA * (8 * bb + 2 * g + 2))
                            wait(dve, recip_row_landed, DMA * (NG * bb + g))
                            dve.reciprocal(recips[:], sums[:]).then_inc(recip_done, 1)
                        if tau - 1 in ATTN_AT and ATTN_AT[tau - 1][0] in live:
                            rel, g = ATTN_AT[tau - 1]
                            bb = b + rel
                            wait(dve, attn_hi, NG * bb + g + 1)
                            dve.scalar_tensor_tensor(r(attnT[:, LO, g, :]), halves[:, g % 2, 0, :],
                                                     vec[:, col["bv"] + g:col["bv"] + g + 1], attnT[:, HI, g, :],
                                                     ALU.add, ALU.subtract).then_inc(attn_lo, 1)

                passes(dve, one_pass)

            @block.gpsimd
            def _(pool):
                def normalise(bb, g):
                    waits(pool, half_done, (recip_done, NG * bb + g + 1))
                    pool.dma_start(rows[32:32 + HG, :], recips[:]).then_inc(recip_row_landed, DMA)
                    waits(pool, half_done, (recip_row_landed, DMA * (NG * bb + g + 1)))
                    for j in range(HG):
                        pool.dma_start(recip_b[HD * j:HD * (j + 1), :],
                                       rows[32 + j:33 + j, :].unsqueeze(1).broadcast_to([1, HD, T])
                                       ).then_inc(recip_b_landed, DMA)
                    for i in range(2):
                        wait(pool, halves_landed[i], 2 * DMA * (8 * bb + 2 * g + 2))
                    a = halves[:, g % 2, 0, :]
                    pool.tensor_tensor(a, a, halves[:, g % 2, 1, :], ALU.add).then_inc(halves_added, 1)
                    wait(pool, halves_added, NG * bb + g + 1)
                    wait(pool, recip_b_landed, HG * DMA * (NG * bb + g + 1))
                    pool.tensor_tensor(a, a, recip_b[:], ALU.mult).then_inc(normed, 1)

                def one_pass(b, live):
                    if -1 in live:
                        normalise(b - 1, 3)
                    if 1 in live and not is_batch(b, -1):
                        moments_and_rows(pool, b + 1, ATTN_NORM, xz, xz)
                    if 0 in live:
                        for g in range(3):
                            if g == 2 and is_batch(b, NB - 1):
                                moments_and_rows(pool, 0, FFN_NORM, staging, xz)
                            normalise(b, g)

                passes(pool, one_pass)

            @block.sync
            def _(sp):
                def one_pass(b, live):
                    for tau in range(64):
                        t, s = tau // SUB, tau % SUB
                        if tau == 0 and 1 in live and not is_batch(b, -1):
                            waits(sp, half_done, (x_turned, KD * (b + 1)))
                            sp.dma_start(xz[:], x_v[bass.ds(b + 1, 1)].rearrange("o p t d -> (o p) t d")
                                         ).then_inc(x_landed, DMA)
                        if is_batch(b, NB - 1) and tau == FIRST_IN_AT:
                            for h in range(NH - HG, NH):
                                sp.wait_ge(stack_landed[h % RING], 3 * DMA * 2 * NB)
                            sp.dma_start(staging[:], x_v[0:1].rearrange("o p t d -> (o p) t d")).then_inc(in_landed[0], DMA)
                            sp.wait_ge(x_turned, KD * NB)
                            for i in range(2):
                                sp.wait_ge(y_stored[i], 2 * DMA)
                            sp.dma_start(xz[:], y_v[0:1].rearrange("o p t d -> (o p) t d")).then_inc(in_landed[0], DMA)
                        for rel, h in STACK_AT.get(tau, ()):
                            if rel not in live:
                                continue
                            bb, g, j = b + rel, h // HG, h % HG
                            waits(sp, half_done, (qk_lo, 2 * KD * bb + 2 * g + 2),
                                  (st_ready, 64 * bb + SUB * (h - RING) + 4))
                            for i, parts in enumerate(STACK_PARTS):
                                sp.dma_start(stack[HD * i:HD * (i + 1), h % RING, :, :],
                                             staging[HD * j:HD * (j + 1), parts, :]).then_inc(stack_landed[h % RING], DMA)
                        if s == 0:
                            rel, h = (0, t - 2) if t >= 2 else (-1, t + NH - 2)
                            if rel in live:
                                bb, j = b + rel, h % HG
                                waits(sp, half_done, (u_copied, NH * bb + h + 1),
                                      (recip_done, NG * bb + h // HG))
                                sp.dma_start(sums[16 * j:16 * j + 16, :], u_sb[2 * HD:VW, h % 2, :]
                                             ).then_inc(sum_landed[h % 2], DMA)
                                g = h // HG
                                if j == 0:
                                    waits(sp, half_done, (attn_lo, NG * bb + g - 1))
                                for c in range(2):
                                    sp.dma_start(halves[HD * j:HD * (j + 1), g % 2, c, :],
                                                 u_sb[HD * c:HD * (c + 1), h % 2, :]).then_inc(halves_landed[h % 2], DMA)
                        for at, kind, rel, n in TURNS:
                            if kind == "neg" and at + 2 == tau and rel in live:
                                bb, p0 = b + rel, 64 * (n % 2)
                                wait(sp, neg_copied, 8 * bb + n + 1)
                                h = 2 * n % RING
                                sp.dma_start(stack[96:97, h:h + 2, 0, :], rows[p0:p0 + 2, :]
                                             ).then_inc(neg_landed[n % 2], DMA)
                        for i, (kind, rel, n, _) in enumerate(UNITS):
                            if kind == "o" and EVACUATED_AT[i] + 1 == tau and rel in live:
                                bb = b + rel
                                waits(sp, half_done, (y_copied, 4 * bb + n + 1))
                                sp.dma_start(y_v[bass.ds(bb, 1), :, n, :].rearrange("o p d -> (o p) d"),
                                             y_sb[:, n % 2, :]).then_inc(y_stored[n % 2], DMA)

                sp.dma_start(bo_b[:], bo.rearrange("(a d) -> a d", a=1).partition_broadcast(P)).then_inc(bias_landed, DMA)
                passes(sp, one_pass)
                for i in range(2):
                    sp.wait_ge(y_stored[i], DMA * 2 * NB)
        part1.close()

        part2 = ExitStack()
        w1_sb = sb(part2, "w1_sb", [P, 2, KD, F])
        w2_sb = sb(part2, "w2_sb", [P, 2, KF, D])
        hid = sb(part2, "hid", [P, 2, 2, T])
        hid_full = sb(part2, "hid_full", [P, 2, T])
        b2_b = sb(part2, "b2_b", [P, D])
        fnT = [xnT, sb(part2, "fnT_odd", [P, 2, KD, T])]
        res.append(sb(part2, "res_odd", [P, TT, D]))
        ACC, HB, TB = ps[0:4], ps[4:6], ps[6:8]
        STATS_AT, TURN_AT = {4: [0], 5: [1], 6: [2], 7: [3]}, {8: [0], 9: [1], 10: [2], 11: [3]}
        STATS_LATE, TURN_LATE = {12: [0, 1], 13: [2, 3]}, {14: [0], 15: [1, 2, 3]}
        PIECES = []
        for c in range(KF):
            PIECES.append((w1.rearrange("(k p) n -> p k n", p=P)[:, :, c * P:(c + 1) * P],
                           [w1_sb[:, a, :, c * P:(c + 1) * P] for a in (HI, LO)],
                           lambda ap: ap.rearrange("p (k n) -> p k n", k=KD)))
            PIECES.append((w2[c * P:(c + 1) * P, :], [w2_sb[:, a, c, :] for a in (HI, LO)], lambda ap: ap))
        raw = [res[1][:, i, :] for i in range(TT)]
        SPLIT_AT = {c: range(4 + 4 * c, min(8 + 4 * c, len(PIECES))) for c in range(len(PIECES) // 4 - 1)}
        fw_landed = [sem(f"fw_landed{i}") for i in range(TT)]
        fw_hi, fw_lo = sem("fw_hi"), sem("fw_lo")

        out_stored = [sem(f"out_stored{i}") for i in range(2)]
        b2_landed, b2_added = sem("b2_landed"), sem("b2_added")
        h_ready, gelu_done, hid_hi, hid_lo = sem("h_ready"), sem("gelu_done"), sem("hid_hi"), sem("hid_lo")
        down_done, acc_read = sem("down_done"), sem("acc_read")

        def stats_at(b, c):
            return (STATS_LATE if isinstance(b, int) and is_batch(b, 0) else STATS_AT).get(c, ())

        def turns_at(b, c):
            return (TURN_LATE if isinstance(b, int) and is_batch(b, 0) else TURN_AT).get(c, ())

        def ffn_passes(eng, one_pass):
            one_pass(0, 0, {0, 1})
            one_pass(1, 1, {-1, 0, 1})
            with eng.Fori(2, NB - 2, 2) as b:
                one_pass(b, 0, {-1, 0, 1})
                one_pass(b + 1, 1, {-1, 0, 1})
            one_pass(NB - 2, 0, {-1, 0, 1})
            one_pass(NB - 1, 1, {-1, 0})
            one_pass(NB, 0, {-1})

        with nc.Block() as block:
            @block.tensor
            def _(pe):
                def one_pass(b, par, live):
                    for c in range(KF):
                        if 0 in live:
                            wait(pe, gelu_done, KF * b + c - 1)
                            for k in range(KD):
                                if k == 0 and is_batch(b, 0):
                                    wait(pe, fw_lo, 2 * c + 1)
                                if c == 0:
                                    wait(pe, fn_lo, KD * b + k + 1)
                                for j, (a, d) in enumerate(PASSES):
                                    last = pe.matmul(HB[c % 2][:], r(w1_sb[:, a, k, c * P:(c + 1) * P]),
                                                     r(fnT[par][:, d, k, :]), start=(k == 0 and j == 0),
                                                     stop=(k == KD - 1 and j == 2))
                            last.then_inc(h_ready, 1)
                        rel, cc = (0, c - 1) if c else (-1, KF - 1)
                        if rel in live:
                            bb = b + rel
                            wait(pe, hid_lo, KF * bb + cc + 1)
                            if is_batch(bb, 0):
                                wait(pe, fw_lo, 2 * cc + 2)
                            for q in range(TT):
                                if cc == 0:
                                    wait(pe, acc_read, TT * bb)
                                for j, (a, d) in enumerate(PASSES):
                                    last = pe.matmul(ACC[q][:], r(hid[:, cc % 2, a, q * P:(q + 1) * P]),
                                                     r(w2_sb[:, d, cc, :]), start=(cc == 0 and j == 0),
                                                     stop=(cc == KF - 1 and j == 2))
                            last.then_inc(down_done, 1)
                        for f in turns_at(b, c) if 1 in live else ():
                            bb = b + 1
                            wait(pe, fz_done, TT * (bb + 1))
                            wait(pe, ft_copied, KD * bb + f - 1)
                            for q in range(TT):
                                last = pe.transpose(TB[f % 2][:, q * P:(q + 1) * P], xz[:, q, f * P:(f + 1) * P], ident[:])
                            last.then_inc(f_turned, 1)
                ffn_passes(pe, one_pass)

            @block.scalar
            def _(act):
                def split(i):
                    src, dst, shape = PIECES[i]
                    act.wait_ge(fw_landed[i % TT], DMA * (i // TT + 1))
                    act.activation(r(dst[HI]), shape(raw[i % TT]), ACT.Copy).then_inc(fw_hi, 1)

                def one_pass(b, par, live):
                    for c in range(KF):
                        if 0 in live:
                            wait(act, h_ready, KF * b + c + 1)
                            wait(act, hid_lo, KF * b + c - 1)
                            act.activation(hid_full[:, c % 2, :], HB[c % 2][:], ACT.Gelu,
                                           bias=vec[:, col["b1"] + c:col["b1"] + c + 1]).then_inc(gelu_done, 1)
                        if is_batch(b, 0):
                            for i in SPLIT_AT.get(c, ()):
                                split(i)
                        for f in turns_at(b, c) if 1 in live else ():
                            bb = b + 1
                            wait(act, f_turned, KD * bb + f + 1)
                            wait(act, fn_lo, KD * bb + f)
                            act.activation(xt[:], TB[f % 2][:], ACT.Identity, bias=mod[:, 1, 1, f, bass.ds(bb, 1)],
                                           scale=mod[:, 1, 0, f, bass.ds(bb, 1)]).then_inc(ft_copied, 1)
                for i in range(SPLIT_AT[0][0]):
                    split(i)
                ffn_passes(act, one_pass)

            @block.vector
            def _(dve):
                def split(i):
                    src, dst, shape = PIECES[i]
                    dve.wait_ge(fw_hi, i + 1)
                    dve.tensor_tensor(r(dst[LO]), shape(raw[i % TT]), dst[HI], ALU.subtract).then_inc(fw_lo, 1)

                def one_pass(b, par, live):
                    for c in range(KF):
                        if 0 in live:
                            wait(dve, gelu_done, KF * b + c + 1)
                            wait(dve, down_done, KF * b + c - 1)
                            dve.tensor_copy(r(hid[:, c % 2, HI, :]), hid_full[:, c % 2, :]).then_inc(hid_hi, 1)
                            wait(dve, hid_hi, KF * b + c + 1)
                            dve.tensor_tensor(r(hid[:, c % 2, LO, :]), hid_full[:, c % 2, :], hid[:, c % 2, HI, :],
                                              ALU.subtract).then_inc(hid_lo, 1)
                        if is_batch(b, 0):
                            for i in SPLIT_AT.get(c, ()):
                                split(i)
                        if c == 0 and -1 in live:
                            wait(dve, down_done, KF * b)
                            wait(dve, b2_added, TT * b)
                            for q in range(TT):
                                dve.tensor_tensor(res[1 - par][:, q, :], ACC[q][:], res[1 - par][:, q, :],
                                                  ALU.add).then_inc(acc_read, 1)
                        for i in stats_at(b, c) if 1 in live else ():
                            bb = b + 1
                            wait(dve, res_done, TT * bb + i + 1)
                            wait(dve, fmv_done, TT * bb)
                            dve.bn_stats(stats[:, i, :], res[1 - par][:, i, :]).then_inc(fstats_done, 1)
                            waits(dve, half_done, (fstats_done, TT * bb + i + 1),
                                  (fz_done, TT * bb))
                            dve.bn_aggr(mean_var[:, i, :], stats[:, i, :]).then_inc(fmv_done, 1)
                        for f in turns_at(b, c) if 1 in live else ():
                            bb = b + 1
                            wait(dve, ft_copied, KD * bb + f + 1)
                            wait(dve, h_ready, KF * b)
                            dve.tensor_copy(r(fnT[1 - par][:, HI, f, :]), xt[:]).then_inc(fn_hi, 1)
                            wait(dve, fn_hi, KD * bb + f + 1)
                            dve.tensor_tensor(r(fnT[1 - par][:, LO, f, :]), xt[:], fnT[1 - par][:, HI, f, :],
                                              ALU.subtract).then_inc(fn_lo, 1)
                for i in range(SPLIT_AT[0][0]):
                    split(i)
                ffn_passes(dve, one_pass)

            @block.gpsimd
            def _(pool):
                pool.wait_ge(bias_landed, DMA)
                pool.wait_ge(b2_landed, DMA)
                for i in range(TT):
                    pool.tensor_tensor(res[0][:, i, :], res[0][:, i, :], b2_b[:], ALU.add).then_inc(b2_added, 1)

                def one_pass(b, par, live):
                    if 1 not in live:
                        return
                    bb, o = b + 1, 1 - par
                    wait(pool, in_landed[o], DMA * (bb + 2 - o))
                    for i in range(TT):
                        pool.tensor_tensor(res[o][:, i, :], res[o][:, i, :], xz[:, i, :], ALU.add).then_inc(summed, 1)
                    for i in range(TT):
                        wait(pool, summed, TT * bb + i + 1)
                        pool.tensor_tensor(res[o][:, i, :], res[o][:, i, :], bo_b[:], ALU.add).then_inc(res_done, 1)
                    moments_and_rows(pool, bb, FFN_NORM, res[o], xz)
                    for i in range(TT):
                        pool.tensor_tensor(res[o][:, i, :], res[o][:, i, :], b2_b[:], ALU.add).then_inc(b2_added, 1)
                ffn_passes(pool, one_pass)

            @block.sync
            def _(sp):
                for i, (src, _, shape) in enumerate(PIECES):
                    wait(sp, fw_lo, i - TT + 1)
                    sp.dma_start(shape(raw[i % TT]), src).then_inc(fw_landed[i % TT], DMA)
                    if i == TT - 1:
                        sp.dma_start(b2_b[:], b2.rearrange("(a d) -> a d", a=1).partition_broadcast(P)
                                     ).then_inc(b2_landed, DMA)
                sp.wait_ge(fw_lo, len(PIECES))

                def one_pass(b, par, live):
                    if -1 in live:
                        bb = b - 1
                        for q in range(TT):
                            waits(sp, half_done, (acc_read, TT * bb + q + 1))
                            sp.dma_start(out_v[bass.ds(bb, 1), :, q, :].rearrange("o p d -> (o p) d"),
                                         res[1 - par][:, q, :]).then_inc(out_stored[1 - par], DMA)
                    if 1 in live:
                        bb, o = b + 1, 1 - par
                        waits(sp, half_done, (out_stored[o], TT * DMA // 2 * (bb - o)),
                              (f_turned, KD * bb))
                        sp.dma_start(res[o][:], x_v[bass.ds(bb, 1)].rearrange("o p t d -> (o p) t d")).then_inc(in_landed[o], DMA)
                        sp.dma_start(xz[:], y_v[bass.ds(bb, 1)].rearrange("o p t d -> (o p) t d")).then_inc(in_landed[o], DMA)
                ffn_passes(sp, one_pass)
                for i in range(2):
                    sp.wait_ge(out_stored[i], TT * DMA * NB // 2)
        part2.close()


_INS = ["x", "cond_1024"] + ["L0_cond_" + n for n in (
    "ln1_w", "ln1_b", "ln2_w", "ln2_b", "wq", "bq", "wk", "bk", "wv", "bv", "wo", "bo",
    "wt_attn", "bt_attn", "wt_ffn", "bt_ffn", "w1", "b1", "w2", "b2")]


def kernel(**inputs):
    import numpy as _np
    import concourse.bacc as _bacc
    from concourse import mybir as _mybir
    from concourse.bass_utils import run_bass_kernel_spmd as _run

    nc = _bacc.Bacc("TRN2", target_bir_lowering=False, num_devices=1)
    arrays, args = {}, []
    for name in _INS:
        a = _np.ascontiguousarray(inputs[name])
        arrays[f"in_{name}_dram"] = a
        args.append(nc.dram_tensor(f"in_{name}_dram", a.shape, _mybir.dt.from_np(a.dtype), kind="ExternalInput").ap())
    shape = arrays["in_x_dram"].shape
    args.append(nc.dram_tensor("attn_out_dram", shape, _mybir.dt.float32, kind="Internal").ap())
    args.append(nc.dram_tensor("out_0_dram", shape, _mybir.dt.float32, kind="ExternalOutput").ap())
    conditioned_layer(nc, *args)
    res = _run(nc, [arrays], core_ids=[0])
    return res.results[0]["out_0_dram"]
```
